# Optimizing a Trainium2 kernel written in Bass

```python
import numpy as np
import jax
import jax.numpy as jnp

def _softmax(x, axis=-1):
    return jax.nn.softmax(x, axis=axis)

def _gelu(x):
    return jax.nn.gelu(x, approximate=True)

def _silu(x):
    return jax.nn.silu(x)

def _sigmoid(x):
    return jax.nn.sigmoid(x)

def _layernorm(x, axis=-1, eps=1e-05):
    m = jnp.mean(x, axis=axis, keepdims=True)
    v = jnp.var(x, axis=axis, keepdims=True)
    return (x - m) / jnp.sqrt(v + eps)

def _scatter_add(tgt, idx, src, axis=0):
    return tgt.at[idx].add(src)

def _segment_sum(src, seg, n):
    return jax.ops.segment_sum(src, seg, n)
kernel_name = 'mk_recurrent_d1_jaxref_r8_341a5f'

def setup_inputs(seed: int=0):
    np.random.seed(seed)
    _w = jnp.asarray

    def _L0_attn_setup():
        import jax, jax.numpy as jnp
        import numpy as np
        import math
        B, S, DM = (1, 256, 512)
        H, HKV, HD = (32, 8, 128)
        EPS = 1e-06
        NEG_INF = -1e+30

        def _alibi_slopes(n_heads: int) -> np.ndarray:
            start = 2 ** (-2 ** (-(math.log2(n_heads) - 3)))
            return np.array([start * start ** i for i in range(n_heads)], dtype=np.float32)

        def _rmsnorm(t, w):
            tf = t.astype(jnp.float32)
            inv = jax.lax.rsqrt(jnp.mean(tf * tf, axis=-1, keepdims=True) + EPS)
            return (tf * inv * w).astype(t.dtype)
        key = jax.random.key(seed)
        ks = jax.random.split(key, 5)
        std = 0.02
        return {'x': jax.random.normal(ks[0], (B, S, DM), dtype=jnp.float32), 'Wq': jax.random.normal(ks[1], (H * HD, DM), dtype=jnp.float32) * std, 'Wk': jax.random.normal(ks[2], (HKV * HD, DM), dtype=jnp.float32) * std, 'Wv': jax.random.normal(ks[3], (HKV * HD, DM), dtype=jnp.float32) * std, 'Wo': jax.random.normal(ks[4], (H * HD, DM), dtype=jnp.float32).T * (std / math.sqrt(2 * 32)), 'q_norm_w': jnp.ones((HD,), dtype=jnp.float32), 'k_norm_w': jnp.ones((HD,), dtype=jnp.float32)}
    _L0_attn_in = _L0_attn_setup()

    def _L0_ffn_setup():
        import jax, jax.numpy as jnp
        import numpy as np
        B, S, H, I = (4, 256, 512, 1376)
        key = jax.random.key(seed)
        k0, k1, k2, k3 = jax.random.split(key, 4)
        scale = 0.02
        return {'x': jax.random.normal(k0, (B, S, H), dtype=jnp.float32), 'w_gate': jax.random.normal(k1, (I, H), dtype=jnp.float32) * scale, 'w_up': jax.random.normal(k2, (I, H), dtype=jnp.float32) * scale, 'w_down': jax.random.normal(k3, (H, I), dtype=jnp.float32) * scale}
    _L0_ffn_in = _L0_ffn_setup()
    _d = {'L0_attn_x': _L0_attn_in['x'], 'L0_attn_Wq': _L0_attn_in['Wq'], 'L0_attn_Wk': _L0_attn_in['Wk'], 'L0_attn_Wv': _L0_attn_in['Wv'], 'L0_attn_Wo': _L0_attn_in['Wo'], 'L0_attn_q_norm_w': _L0_attn_in['q_norm_w'], 'L0_attn_k_norm_w': _L0_attn_in['k_norm_w'], 'L0_ffn_w_gate': _L0_ffn_in['w_gate'], 'L0_ffn_w_up': _L0_ffn_in['w_up'], 'L0_ffn_w_down': _L0_ffn_in['w_down']}
    _x0 = _d['L0_attn_x']
    _d['L0_attn_x'] = jax.random.normal(jax.random.fold_in(jax.random.key(seed), 1), (2, 1024, 512), dtype=_x0.dtype)
    del _x0
    return _d

def reference(L0_attn_x, L0_attn_Wq, L0_attn_Wk, L0_attn_Wv, L0_attn_Wo, L0_attn_q_norm_w, L0_attn_k_norm_w, L0_ffn_w_gate, L0_ffn_w_up, L0_ffn_w_down):

    def _L0_attn_ref(x, Wq, Wk, Wv, Wo, q_norm_w, k_norm_w):
        import jax, jax.numpy as jnp
        import numpy as np
        import math
        B, S, DM = (1, 256, 512)
        H, HKV, HD = (32, 8, 128)
        EPS = 1e-06
        NEG_INF = -1e+30

        def _alibi_slopes(n_heads: int) -> np.ndarray:
            start = 2 ** (-2 ** (-(math.log2(n_heads) - 3)))
            return np.array([start * start ** i for i in range(n_heads)], dtype=np.float32)

        def _rmsnorm(t, w):
            tf = t.astype(jnp.float32)
            inv = jax.lax.rsqrt(jnp.mean(tf * tf, axis=-1, keepdims=True) + EPS)
            return (tf * inv * w).astype(t.dtype)
        b, s, _ = x.shape
        G = H // HKV
        q = (x @ Wq.T).reshape(b, s, H, HD).transpose(0, 2, 1, 3)
        k = (x @ Wk.T).reshape(b, s, HKV, HD).transpose(0, 2, 1, 3)
        v = (x @ Wv.T).reshape(b, s, HKV, HD).transpose(0, 2, 1, 3)
        q = _rmsnorm(q, q_norm_w)
        k = _rmsnorm(k, k_norm_w)
        qg = q.reshape(b, HKV, G, s, HD)
        scores = jnp.einsum('bkgqd,bksd->bkgqs', qg, k) / math.sqrt(HD)
        slopes = jnp.asarray(_alibi_slopes(H)).reshape(HKV, G)
        pos = jnp.arange(s, dtype=jnp.float32)
        rel = pos[None, :] - pos[:, None]
        bias = jnp.where(rel > 0, NEG_INF, slopes[:, :, None, None] * rel)
        attn = jax.nn.softmax(scores + bias[None], axis=-1)
        out = jnp.einsum('bkgqs,bksd->bkgqd', attn, v)
        out = out.reshape(b, H, s, HD).transpose(0, 2, 1, 3).reshape(b, s, H * HD)
        return out @ Wo.T

    def _L0_ffn_ref(x, w_gate, w_up, w_down):
        import jax, jax.numpy as jnp
        import numpy as np
        B, S, H, I = (4, 256, 512, 1376)
        gate = jnp.einsum('bsh,ih->bsi', x, w_gate)
        up = jnp.einsum('bsh,ih->bsi', x, w_up)
        inter = jax.nn.silu(gate) * up
        return jnp.einsum('bsi,hi->bsh', inter, w_down)
    x = L0_attn_x
    xn = _layernorm(x, axis=-1)
    s = _L0_attn_ref(xn, L0_attn_Wq, L0_attn_Wk, L0_attn_Wv, L0_attn_Wo, L0_attn_q_norm_w, L0_attn_k_norm_w)
    g = _silu(_L0_ffn_ref(xn, L0_ffn_w_gate, L0_ffn_w_up, L0_ffn_w_down))
    x = x + s * g
    return x

_drawn_inputs = setup_inputs


def setup_inputs(seed=0):
    import zlib

    import numpy as np

    out = dict(_drawn_inputs(seed))
    spreads = {'L0_attn_q_norm_w': (1.0, 0.6), 'L0_attn_k_norm_w': (1.0, 0.6)}
    factors = {'L0_attn_Wq': 8.0,
     'L0_attn_Wk': 8.0,
     'L0_attn_Wv': 8.0,
     'L0_attn_Wo': 8.0,
     'L0_ffn_w_gate': 8.0,
     'L0_ffn_w_up': 8.0,
     'L0_ffn_w_down': 8.0}
    for name, (base, spread) in spreads.items():
        noise = np.random.default_rng([zlib.crc32(name.encode()), seed]).standard_normal(out[name].shape)
        drawn = base * np.exp(spread * noise) if base else spread * noise
        out[name] = jnp.asarray(drawn.astype(out[name].dtype))
    for name, factor in factors.items():
        out[name] = (out[name] * factor).astype(out[name].dtype)
    return out
```

```python
from contextlib import ExitStack

import numpy as np

import concourse.bass as bass
from concourse import mybir

F32 = mybir.dt.float32
F32R = mybir.dt.float32r
I32 = mybir.dt.int32
ALU = mybir.AluOpType
ACT = mybir.ActivationFunctionType
AX = mybir.AxisListType

P = 128
B, S, D = 2, 1024, 512
TILES = S // P
DC = D // P
H, HKV = 32, 8
G = H // HKV
UNITS = HKV
INNER = 1376
FC = -(-INNER // P)
HALVES = 2
CHUNKS = HALVES * FC
HT = TILES // HALVES
BANK = 512
KV = 2 * P
NQ = DC * D
NKV = DC * KV
NGU = 2 * DC * P
NCH = NGU + D
MASK = 2.0 ** 110
LN_EPS, RMS_EPS = 1e-5, 1e-6
RSQRT_SEED = float(0x5F3759DF)
NEWTON = 3
CHAIN = 2 + 4 * NEWTON

HEAD_CHUNKS = [-(-(i + 1) * P // BANK) for i in range(TILES)]
SCORE_AT = [G * sum(HEAD_CHUNKS[:i]) for i in range(TILES + 1)]
SCORES = SCORE_AT[TILES]
TURNS = TILES * (TILES + 1) // 2
BEFORE = [TILES] + list(range(1, TILES))
TURN_AT = [sum(BEFORE[1:i + 1]) - BEFORE[i] for i in range(TILES)] + [TURNS - TILES]
RING, LOWS = TURNS + 3 * TILES, TURNS + 2 * TILES
RING_AT, LOW_AT = [3 - 2 - TILES], [2 - TILES]
for _i in range(TILES):
    RING_AT.append(RING_AT[-1] + BEFORE[_i] + 3)
    LOW_AT.append(LOW_AT[-1] + BEFORE[_i] + 2)
STEADY_LOW = list(LOW_AT)
RING_AT[TILES] -= 2
LOW_AT[TILES] -= 2
RBANKS = 3
SLOTS = 4
LAG = 2


def ring_low(r, first, ending):
    if first and r < 2:
        return r
    if ending and r >= RING_AT[TILES]:
        j = r - RING_AT[TILES]
        return LOW_AT[TILES] + j if j < TILES else None
    if r < RING_AT[0]:
        low = ring_low(r + RING, False, False)
        return None if low is None else low - LOWS
    i = max(k for k in range(TILES) if RING_AT[k] <= r)
    j = r - RING_AT[i]
    if j == BEFORE[i]:
        return None
    return LOW_AT[i] + j - (j > BEFORE[i])


def shape_of_step(i, first):
    chunks = G * HEAD_CHUNKS[i] if i < TILES else 0
    turns = 0 if first and i == 0 else TILES if i == TILES else BEFORE[i]
    return chunks, turns, max(chunks, turns + LAG if turns else 0)


def build(nc, x, w_qkv, w_o, w_ffn, q_norm, k_norm, rel, slopes, inv_slopes, ident_in, out):
    ctx = ExitStack()
    with ctx:
        def sb(name, shape, dt=F32):
            return ctx.enter_context(nc.sbuf_tensor(name, shape, dt))

        def psum(name, shape):
            return ctx.enter_context(nc.psum_tensor(name, shape, F32))

        def sem(name):
            return ctx.enter_context(nc.semaphore(name))

        xT_hi, xT_lo = sb("xT_hi", [P, DC, S], F32R), sb("xT_lo", [P, DC, S], F32R)
        y = sb("y", [P, TILES, D])
        qkv_raw, o_raw = sb("qkv_raw", [P, NQ + NKV]), sb("o_raw", [P, G * D])
        qkv_hi, qkv_lo = sb("qkv_hi", [P, NQ + NKV], F32R), sb("qkv_lo", [P, NQ + NKV], F32R)
        o_hi, o_lo = sb("o_hi", [P, G, D], F32R), sb("o_lo", [P, G, D], F32R)
        kT_hi, kT_lo = sb("kT_hi", [P, S], F32R), sb("kT_lo", [P, S], F32R)
        v_hi, v_lo = sb("v_hi", [P, TILES, P], F32R), sb("v_lo", [P, TILES, P], F32R)
        qT_hi, qT_lo = sb("qT_hi", [P, 2, G, P], F32R), sb("qT_lo", [P, 2, G, P], F32R)
        probs = [sb("probs0", [P, G, S - P]), sb("probs1", [P, G, S])]
        pT_hi, pT_lo = sb("pT_hi", [P, SLOTS, G * P], F32R), sb("pT_lo", [P, SLOTS, G * P], F32R)
        attT = sb("attT", [P, G * P])
        attT_hi, attT_lo = sb("attT_hi", [P, G, P], F32R), sb("attT_lo", [P, G, P], F32R)
        recT = sb("recT", [P, G * P])
        qk_sq = sb("qk_sq", [P, (G + 1) * P])
        qk = sb("qk", [P, G + 1, P])
        v_nat = sb("v_nat", [P, 2, P])
        rel_sb, ident = sb("rel_sb", [P, S]), sb("ident", [P, P])
        slope, inv_slope = sb("slope", [P, G]), sb("inv_slope", [P, G + 1])
        norm_w, wcol = sb("norm_w", [P, 2]), sb("wcol", [P, 1])
        low_min = sb("low_min", [P, 2, G, 2])
        row_sum, rec = sb("row_sum", [P, 2, G]), sb("rec", [P, G])
        sq_sum, rs_x, rs_a, rq = sb("sq_sum", [P, 8]), sb("rs_x", [P, 8]), sb("rs_a", [P, 8]), sb("rq", [P, 8])
        rs_y = sb("rs_y", [P, 8])
        stats, mv = sb("stats", [P, TILES, 6]), sb("mv", [P, TILES, 2])

        f_raw = [qkv_raw[:, k * NCH:(k + 1) * NCH] for k in range(2)]
        f_hi = [qkv_hi[:, k * NCH:(k + 1) * NCH] for k in range(2)]
        f_lo = [qkv_lo[:, k * NCH:(k + 1) * NCH] for k in range(2)]
        probs0 = probs[0][:, :, :].rearrange("p g n -> p (g n)")
        f_silu = [probs0[:, k * BANK:(k + 1) * BANK] for k in range(2)]
        f_prod = [probs0[:, (2 + k) * BANK:(3 + k) * BANK] for k in range(2)]
        f_gate = [probs0[:, (4 + k) * BANK:(5 + k) * BANK] for k in range(2)]
        x_again = probs[1][:, :, :].rearrange("p g n -> p (g n)").rearrange("p (t d) -> p t d", d=D)

        qkv_ps = psum("qkv_ps", [P, 2 * BANK])
        score_ps = psum("score_ps", [P, 2, BANK])
        ring_ps = psum("ring_ps", [P, RBANKS, BANK])
        out_ps = psum("out_ps", [P, BANK])
        gate_ps = [score_ps[:, k, :] for k in range(2)]
        up_ps = [qkv_ps[:, k * BANK:(k + 1) * BANK] for k in range(2)]
        down_ps = [ring_ps[:, k, :] for k in range(RBANKS)] + [out_ps[:, :]]
        assert HT == len(down_ps)

        consts_in, w_in = sem("consts_in"), sem("w_in")
        x_in, x_again_in = sem("x_in"), sem("x_again_in")
        qkv_in, o_in, slope_in, inv_in = sem("qkv_in"), sem("o_in"), sem("slope_in"), sem("inv_in")
        f_in = [sem("f_in0"), sem("f_in1")]
        stats_done, mv_done = sem("stats_done"), sem("mv_done")
        xn_done, xT_turned, xT_high, xT_low = sem("xn_done"), sem("xT_turned"), sem("xT_high"), sem("xT_low")
        y_zero = sem("y_zero")
        w_high, w_split, o_high, o_split = sem("w_high"), sem("w_split"), sem("o_high"), sem("o_split")
        projected, squared, summed, rq_done = sem("projected"), sem("squared"), sem("summed"), sem("rq_done")
        qk_done, v_staged, v_high, v_split = sem("qk_done"), sem("v_staged"), sem("v_high"), sem("v_split")
        scored, biased, exped = sem("scored"), sem("biased"), sem("exped")
        ring_full, ring_high, ring_lowd = sem("ring_full"), sem("ring_high"), sem("ring_lowd")
        weighed, rec_done = sem("weighed"), sem("rec_done")
        att_done, att_high, att_split = sem("att_done"), sem("att_high"), sem("att_split")
        out_proj, y_added = sem("out_proj"), sem("y_added")
        pool_chain = sem("pool_chain")
        f_gu_high, f_d_high = sem("f_gu_high"), sem("f_d_high")
        f_gu_split, f_d_split = sem("f_gu_split"), sem("f_d_split")
        f_gu_done, f_silu_done, f_prod_done = sem("f_gu_done"), sem("f_silu_done"), sem("f_prod_done")
        f_high, f_low, f_down = sem("f_high"), sem("f_low"), sem("f_down")
        gate_done, gated, out_ready, stored = sem("gate_done"), sem("gated"), sem("out_ready"), sem("stored")
        sp_passed, dve_passed, pool_passed, wcol_done = sem("sp_passed"), sem("dve_passed"), sem("pool_passed"), sem("wcol_done")

        block = ctx.enter_context(nc.Block())

        def units(eng, b, body):
            body(b * UNITS, True, False)
            with eng.Fori(1, UNITS - 1) as g:
                body(b * UNITS + g, False, False)
            body(b * UNITS + UNITS - 1, False, True)

        def tile(U, i):
            return U * TILES + i + 1

        @block.sync
        def _(sp):
            sp.dma_start(ident[:, :], ident_in).then_inc(consts_in, 16)
            sp.dma_start(rel_sb[:, :], rel).then_inc(consts_in, 16)
            sp.dma_start(norm_w[:, 0:1], q_norm).then_inc(w_in, 16)
            sp.dma_start(norm_w[:, 1:2], k_norm).then_inc(w_in, 16)

            def load_unit(g):
                sp.dma_start(qkv_raw[:, :], w_qkv[bass.ds(g, 1), :, :].rearrange("a p n -> p (a n)")).then_inc(qkv_in, 16)

            def load_o(g):
                sp.dma_start(o_raw[:, :], w_o[bass.ds(g, 1), :, :].rearrange("a p n -> p (a n)")).then_inc(o_in, 16)

            def load_inv(g):
                sp.dma_start(inv_slope[:, :], inv_slopes[bass.ds(g, 1), :, :].rearrange("a p n -> p (a n)")).then_inc(inv_in, 16)

            def load_slope(g):
                sp.dma_start(slope[:, :], slopes[bass.ds(g, 1), :, :].rearrange("a p n -> p (a n)")).then_inc(slope_in, 16)

            with sp.Fori(0, B) as b:
                x_rows = x[bass.ds(b, 1), :, :].rearrange("a (t p) d -> p (a t) d", p=P)
                sp.dma_start(y[:, :, :], x_rows).then_inc(x_in, 16)
                load_unit(0)
                load_o(0)
                load_inv(0)
                load_slope(0)
                with sp.Fori(0, UNITS - 1) as g:
                    U = b * UNITS + g
                    sp.wait_ge(w_split, U + 1)
                    sp.sem_inc(sp_passed, 1)
                    load_unit(g + 1)
                    sp.wait_ge(o_split, U + 1)
                    sp.sem_inc(sp_passed, 1)
                    load_o(g + 1)
                    sp.wait_ge(rq_done, (U + 1) * TILES)
                    sp.sem_inc(sp_passed, 1)
                    load_inv(g + 1)
                    sp.wait_ge(biased, (U + 1) * SCORES)
                    sp.sem_inc(sp_passed, 1)
                    load_slope(g + 1)
                last = b * UNITS + UNITS
                for c in range(CHUNKS):
                    if c == 0:
                        sp.wait_ge(w_split, last)
                    if c >= 2:
                        sp.wait_ge(f_d_split, b * CHUNKS + c - 1)
                        sp.sem_inc(sp_passed, 1)
                    if c == 2:
                        sp.wait_ge(weighed, last * TURNS)
                        sp.sem_inc(sp_passed, 1)
                        sp.dma_start(x_again[:, :, :], x_rows).then_inc(x_again_in, 16)
                    sp.dma_start(f_raw[c % 2], w_ffn[c % FC]).then_inc(f_in[c % 2], 16)
                for t in range(TILES):
                    sp.wait_ge(out_ready, b * TILES + t + 1)
                    sp.sem_inc(sp_passed, 1)
                    sp.dma_start(out[bass.ds(b, 1), t * P:(t + 1) * P, :].rearrange("a p d -> p (a d)"),
                                 y[:, t, :]).then_inc(stored, 16)
                sp.wait_ge(stored, (b + 1) * TILES * 16)
                sp.sem_inc(sp_passed, 1)

        @block.tensor
        def _(pe):
            def ring_free(U, r, first, ending):
                q = r - RBANKS
                if first and q < 0:
                    return
                low = ring_low(q, first, ending)
                if low is None:
                    pe.wait_ge(ring_high, U * RING + q + 1)
                else:
                    pe.wait_ge(ring_lowd, U * LOWS + low + 1)

            def project(U, i, first):
                if not first:
                    pe.wait_ge(qk_done, tile(U, i) - 1)
                    pe.wait_ge(v_staged, tile(U, i) - 1)
                if i == 0:
                    pe.wait_ge(w_split, U + 1)
                for c in range(DC):
                    for xT, w in ((xT_hi, qkv_hi), (xT_hi, qkv_lo), (xT_lo, qkv_hi)):
                        a = xT[:, c, i * P:(i + 1) * P]
                        go, end = c == 0 and xT is xT_hi and w is qkv_hi, c == DC - 1 and xT is xT_lo
                        pe.matmul(qkv_ps[:, 0:BANK], a, w[:, c * D:(c + 1) * D], start=go, stop=end)
                        mm = pe.matmul(qkv_ps[:, BANK:BANK + KV], a, w[:, NQ + c * KV:NQ + (c + 1) * KV],
                                       start=go, stop=end)
                mm.then_inc(projected, 1)

            def turn_q(U, i, r, first, ending, t):
                ring_free(U, r, first, ending)
                pe.wait_ge(qk_done, t)
                for h in range(G):
                    tr = pe.transpose(ring_ps[:, r % RBANKS, h * P:(h + 1) * P], qk[:, h, :], ident[:, :])
                tr.then_inc(ring_full, 1)

            def turn_k(U, i, r, first, ending):
                ring_free(U, r, first, ending)
                pe.transpose(ring_ps[:, r % RBANKS, 0:P], qk[:, G, :], ident[:, :]).then_inc(ring_full, 1)

            def scores(U, i, k, first):
                n = SCORE_AT[i] + k
                h, part = k // HEAD_CHUNKS[i], k % HEAD_CHUNKS[i]
                lo, hi = part * BANK, min((part + 1) * BANK, (i + 1) * P)
                if k == 0:
                    low = 1 if first and i == 0 else STEADY_LOW[i] - 1
                    pe.wait_ge(ring_lowd, U * LOWS + low + 1)
                if not (first and n < 2):
                    pe.wait_ge(biased, U * SCORES + n - 1)
                for q, kt in ((qT_hi, kT_hi), (qT_hi, kT_lo), (qT_lo, kT_hi)):
                    mm = pe.matmul(score_ps[:, n % 2, 0:hi - lo], q[:, i % 2, h, :], kt[:, lo:hi],
                                   start=(q is qT_hi and kt is kT_hi), stop=(q is qT_lo))
                mm.then_inc(scored, 1)

            def turn_probs(U, i, j, first, ending):
                r, p = RING_AT[i] + j, (i - 1) % TILES
                ring_free(U, r, first, ending)
                for h in range(G):
                    if j == 0:
                        pe.wait_ge(exped, (U * TILES + i - 1) * G + h + 1)
                    tr = pe.transpose(ring_ps[:, r % RBANKS, h * P:(h + 1) * P],
                                      probs[p % 2][:, h, j * P:(j + 1) * P], ident[:, :])
                tr.then_inc(ring_full, 1)

            def turn_rec(U, i, turns, first, ending):
                r = RING_AT[i] + turns
                ring_free(U, r, first, ending)
                pe.wait_ge(rec_done, U * TILES + i)
                for h in range(G):
                    tr = pe.transpose(ring_ps[:, r % RBANKS, h * P:(h + 1) * P],
                                      rec[:, h:h + 1].to_broadcast([P, P]), ident[:, :])
                tr.then_inc(ring_full, 1)

            def weigh(U, i, j, turns, first):
                if j == 0:
                    pe.wait_ge(v_split, U * TILES + i)
                    if not (first and i < 2):
                        pe.wait_ge(y_added, U * TILES + i - 1)
                pe.wait_ge(ring_lowd, U * LOWS + LOW_AT[i] + j + 1)
                slot = (TURN_AT[i] + j) % SLOTS
                for v, pt in ((v_hi, pT_hi), (v_hi, pT_lo), (v_lo, pT_hi)):
                    mm = pe.matmul(out_ps[:, :], v[:, j, :], pt[:, slot, :],
                                   start=(j == 0 and v is v_hi and pt is pT_hi),
                                   stop=(j == turns - 1 and v is v_lo))
                mm.then_inc(weighed, 1)

            def out_project(U, i, wait_w):
                if wait_w:
                    pe.wait_ge(o_split, U + 1)
                pe.wait_ge(att_split, U * TILES + i - 1)
                for h in range(G):
                    for a, w in ((attT_hi, o_hi), (attT_hi, o_lo), (attT_lo, o_hi)):
                        mm = pe.matmul(out_ps[:, :], a[:, h, :], w[:, h, :],
                                       start=(h == 0 and a is attT_hi and w is o_hi),
                                       stop=(h == G - 1 and a is attT_lo))
                mm.then_inc(out_proj, 1)

            def step(U, i, first, last):
                ending = i >= TILES
                ahead = not (last and i >= TILES - 1)
                if ahead:
                    project(U if i < TILES - 1 else U + 1, (i + 1) % TILES, False)
                if not (first and i < 2):
                    out_project(U, i, i == 2)
                if i > TILES:
                    return
                chunks, turns, slots = shape_of_step(i, first)
                for k in range(slots):
                    if k < chunks:
                        scores(U, i, k, first)
                    if k < turns:
                        turn_probs(U, i, k, first, ending)
                    if turns and k == turns:
                        turn_rec(U, i, turns, first, ending)
                    if ahead and turns and k == turns + 1:
                        turn_q(U, i, RING_AT[i] + BEFORE[i] + 1, first, ending, tile(U, i + 1))
                    if 0 <= k - LAG < turns:
                        weigh(U, i, k - LAG, turns, first)
                if ahead:
                    r = RING_AT[i] + BEFORE[i] + 1
                    if not turns:
                        turn_q(U, i, r, first, ending, tile(U, i + 1))
                    turn_k(U, i, r + 1, first, ending)

            def unit(U, first, last):
                if first:
                    project(U, 0, True)
                    turn_q(U, 0, 0, True, False, tile(U, 0))
                    turn_k(U, 0, 1, True, False)
                for i in range(TILES + 2 if last else TILES):
                    step(U, i, first, last)

            pe.wait_ge(consts_in, 32)
            with pe.Fori(0, B) as b:
                for t in range(TILES):
                    pe.wait_ge(xn_done, b * TILES + t + 1)
                    if t >= RBANKS:
                        pe.wait_ge(xT_low, b * TILES + t - RBANKS + 1)
                    for c in range(DC):
                        tr = pe.transpose(ring_ps[:, t % RBANKS, c * P:(c + 1) * P], y[:, t, c * P:(c + 1) * P], ident[:, :])
                    tr.then_inc(xT_turned, 1)
                pe.wait_ge(xT_low, (b + 1) * TILES)
                units(pe, b, unit)

                def gate_up(c):
                    n, k, half = b * CHUNKS + c, c % 2, c // FC
                    pe.wait_ge(f_gu_split, n + 1)
                    if c >= 2:
                        pe.wait_ge(f_prod_done, n - 1)
                    for part, acc in ((0, gate_ps[k]), (1, up_ps[k])):
                        for d in range(DC):
                            for w, xT in ((f_hi, xT_hi), (f_hi, xT_lo), (f_lo, xT_hi)):
                                at = (part * DC + d) * P
                                mm = pe.matmul(acc, w[k][:, at:at + P], xT[:, d, half * BANK:(half + 1) * BANK],
                                               start=(d == 0 and w is f_hi and xT is xT_hi),
                                               stop=(d == DC - 1 and w is f_lo))
                    mm.then_inc(f_gu_done, 1)

                def down(c):
                    n, k = b * CHUNKS + c, c % 2
                    pe.wait_ge(f_d_split, n + 1)
                    pe.wait_ge(f_low, n + 1)
                    if c == 0:
                        pe.wait_ge(y_added, (b + 1) * UNITS * TILES)
                    if c == FC:
                        pe.wait_ge(gate_done, b * TILES + HT)
                    for t in range(HT):
                        for a, w in ((pT_hi, f_hi), (pT_hi, f_lo), (pT_lo, f_hi)):
                            mm = pe.matmul(down_ps[t], a[:, k, t * P:(t + 1) * P], w[k][:, NGU:NCH],
                                           start=(c % FC == 0 and a is pT_hi and w is f_hi),
                                           stop=(c % FC == FC - 1 and a is pT_lo))
                    mm.then_inc(f_down, 1)

                for c in range(CHUNKS):
                    gate_up(c)
                    if c:
                        down(c - 1)
                down(CHUNKS - 1)

        @block.scalar
        def _(act):
            def square(U, i, t, first):
                act.wait_ge(projected, t)
                if not first:
                    act.wait_ge(summed, t - 1)
                act.activation(qk_sq[:, :], qkv_ps[:, 0:(G + 1) * P], ACT.Square).then_inc(squared, 1)

            def stage_v(U, i, t, early):
                if not early:
                    act.wait_ge(v_split, t - 2)
                act.activation(v_nat[:, i % 2, :], qkv_ps[:, BANK + P:BANK + KV], ACT.Copy).then_inc(v_staged, 1)

            def high_q(U, i, r):
                act.wait_ge(ring_full, U * RING + r + 1)
                act.activation(qT_hi[:, i % 2, :, :].rearrange("p g n -> p (g n)"), ring_ps[:, r % RBANKS, :],
                               ACT.Copy, scale=wcol[:, 0:1]).then_inc(ring_high, 1)

            def high_k(U, i, r):
                act.wait_ge(ring_full, U * RING + r + 1)
                act.activation(kT_hi[:, i * P:(i + 1) * P], ring_ps[:, r % RBANKS, 0:P], ACT.Copy).then_inc(ring_high, 1)

            def exp(U, i, h):
                act.wait_ge(biased, U * SCORES + SCORE_AT[i] + (h + 1) * HEAD_CHUNKS[i])
                row = probs[i % 2][:, h, 0:(i + 1) * P]
                act.activation(row, row, ACT.Exp, scale=-1.0, bias=low_min[:, i % 2, h, HEAD_CHUNKS[i] - 1:HEAD_CHUNKS[i]],
                               accum_out=row_sum[:, i % 2, h:h + 1]).then_inc(exped, 1)

            def high_probs(U, i, j, first):
                r, n = RING_AT[i] + j, TURN_AT[i] + j
                act.wait_ge(ring_full, U * RING + r + 1)
                if not (first and n < SLOTS):
                    act.wait_ge(weighed, U * TURNS + n - SLOTS + 1)
                act.activation(pT_hi[:, n % SLOTS, :], ring_ps[:, r % RBANKS, :], ACT.Copy).then_inc(ring_high, 1)

            def copy_rec(U, i, turns):
                r = RING_AT[i] + turns
                act.wait_ge(ring_full, U * RING + r + 1)
                act.activation(recT[:, :], ring_ps[:, r % RBANKS, :], ACT.Copy).then_inc(ring_high, 1)

            def high_att(U, i):
                act.wait_ge(att_done, U * TILES + i - 1)
                act.activation(attT_hi[:, :, :].rearrange("p g n -> p (g n)"), attT[:, :], ACT.Copy).then_inc(att_high, 1)

            def high_o(U, used):
                act.wait_ge(o_in, (U + 1) * 16)
                if used:
                    act.wait_ge(out_proj, U * TILES)
                act.activation(o_hi[:, :, :].rearrange("p g n -> p (g n)"), o_raw[:, :], ACT.Copy).then_inc(o_high, 1)

            def step(U, i, first, last):
                ahead = not (last and i >= TILES - 1)
                if not (first and i < 2):
                    high_att(U, i)
                if i > TILES:
                    return
                if ahead:
                    square(U, i + 1, tile(U, i + 1), False)
                    stage_v(U, (i + 1) % TILES, tile(U, i + 1), first and i == 0)
                chunks, turns, slots = shape_of_step(i, first)
                for k in range(slots + 1):
                    if k < turns:
                        high_probs(U, i, k, first)
                    if turns and k == turns:
                        copy_rec(U, i, turns)
                    if ahead and turns and k == turns + 1:
                        high_q(U, (i + 1) % TILES, RING_AT[i] + BEFORE[i] + 1)
                    if 1 <= k <= chunks and k % HEAD_CHUNKS[i] == 0:
                        exp(U, i, k // HEAD_CHUNKS[i] - 1)
                    if k == 1 and i == 1 and not first:
                        high_o(U, True)
                if ahead:
                    r = RING_AT[i] + BEFORE[i] + 1
                    if not turns:
                        high_q(U, i + 1, r)
                    high_k(U, (i + 1) % TILES, r + 1)

            def unit(U, first, last):
                if first:
                    high_o(U, False)
                    square(U, 0, tile(U, 0), True)
                    stage_v(U, 0, tile(U, 0), True)
                    high_q(U, 0, 0)
                    high_k(U, 0, 1)
                for i in range(TILES + 2 if last else TILES):
                    step(U, i, first, last)

            act.wait_ge(wcol_done, 1)
            with act.Fori(0, B) as b:
                for t in range(TILES):
                    act.wait_ge(xT_turned, b * TILES + t + 1)
                    act.activation(xT_hi[:, :, t * P:(t + 1) * P],
                                   ring_ps[:, t % RBANKS, :].rearrange("p (c n) -> p c n", c=DC), ACT.Copy).then_inc(xT_high, 1)
                units(act, b, unit)
                for c in range(CHUNKS):
                    n, k = b * CHUNKS + c, c % 2
                    act.wait_ge(f_gu_done, n + 1)
                    act.activation(f_silu[k], gate_ps[k], ACT.Silu).then_inc(f_silu_done, 1)
                    act.wait_ge(f_prod_done, n + 1)
                    if c >= 2:
                        act.wait_ge(f_down, n - 1)
                    act.activation(pT_hi[:, k, :], f_prod[k], ACT.Copy).then_inc(f_high, 1)
                    if c in (FC, CHUNKS - 1):
                        half = 0 if c == FC else 1
                        act.wait_ge(f_down, b * CHUNKS + (half + 1) * FC)
                        for t in range(HT):
                            m = half * HT + t
                            if m >= 2:
                                act.wait_ge(gated, b * TILES + m - 1)
                            act.activation(f_gate[m % 2], down_ps[t], ACT.Silu).then_inc(gate_done, 1)

        @block.vector
        def _(dve):
            def sum_squares(U, t, first):
                dve.wait_ge(squared, t)
                if not first:
                    dve.wait_ge(rq_done, t - 1)
                dve.tensor_reduce(sq_sum[:, 0:G + 1], qk_sq[:, :].rearrange("p (g n) -> p g n", g=G + 1),
                                  AX.X, ALU.add).then_inc(summed, 1)

            def scale_qk(U, t):
                dve.wait_ge(rq_done, t)
                dve.wait_ge(v_staged, t)
                dve.tensor_tensor(out=qk[:, :, :], in0=qkv_ps[:, 0:(G + 1) * P].rearrange("p (g n) -> p g n", g=G + 1),
                                  in1=rq[:, 0:G + 1].unsqueeze(2).to_broadcast([P, G + 1, P]), op=ALU.mult).then_inc(qk_done, 1)

            def low_q(U, i, r):
                dve.wait_ge(ring_high, U * RING + r + 1)
                dve.scalar_tensor_tensor(out=qT_lo[:, i % 2, :, :].rearrange("p g n -> p (g n)"), in0=ring_ps[:, r % RBANKS, :],
                                         scalar=wcol[:, 0:1], in1=qT_hi[:, i % 2, :, :].rearrange("p g n -> p (g n)").bitcast(F32),
                                         op0=ALU.mult, op1=ALU.subtract).then_inc(ring_lowd, 1)

            def low_k(U, i, r):
                dve.wait_ge(ring_high, U * RING + r + 1)
                dve.tensor_tensor(out=kT_lo[:, i * P:(i + 1) * P], in0=ring_ps[:, r % RBANKS, 0:P],
                                  in1=kT_hi[:, i * P:(i + 1) * P].bitcast(F32), op=ALU.subtract).then_inc(ring_lowd, 1)

            def bias(U, i, k):
                n = SCORE_AT[i] + k
                h, part = k // HEAD_CHUNKS[i], k % HEAD_CHUNKS[i]
                lo, hi = part * BANK, min((part + 1) * BANK, (i + 1) * P)
                if k == 0 and i == 0:
                    dve.wait_ge(slope_in, (U + 1) * 16)
                if part:
                    dve.wait_ge(biased, U * SCORES + n)
                dve.wait_ge(scored, U * SCORES + n + 1)
                dve.sem_inc(dve_passed, 1)
                at = S - (i + 1) * P + lo
                dve.tensor_tensor_reduce(
                    out=probs[i % 2][:, h, lo:hi], in0=score_ps[:, n % 2, 0:hi - lo], in1=rel_sb[:, at:at + hi - lo],
                    scale=slope[:, h:h + 1], scalar=low_min[:, i % 2, h, 0:1] if part else 3.0e38,
                    op0=ALU.add, op1=ALU.min, accum_out=low_min[:, i % 2, h, part:part + 1]).then_inc(biased, 1)

            def low_probs(U, i, j):
                r, n = RING_AT[i] + j, TURN_AT[i] + j
                dve.wait_ge(ring_high, U * RING + r + 1)
                dve.tensor_tensor(out=pT_lo[:, n % SLOTS, :], in0=ring_ps[:, r % RBANKS, :],
                                  in1=pT_hi[:, n % SLOTS, :].bitcast(F32), op=ALU.subtract).then_inc(ring_lowd, 1)

            def reciprocal(U, i):
                dve.wait_ge(exped, (U * TILES + i) * G)
                dve.reciprocal(rec[:, :], row_sum[:, (i - 1) % 2, :]).then_inc(rec_done, 1)

            def normalise(U, i):
                dve.wait_ge(weighed, U * TURNS + (TURN_AT[i] if i <= TILES else TURNS))
                r = (RING_AT[TILES - 1] + BEFORE[TILES - 1] - RING if i == 0
                     else RING_AT[TILES] + TILES if i == TILES + 1 else RING_AT[i - 1] + BEFORE[i - 1])
                dve.wait_ge(ring_high, U * RING + r + 1)
                dve.tensor_tensor(out=attT[:, :], in0=out_ps[:, :], in1=recT[:, :], op=ALU.mult).then_inc(att_done, 1)

            def add_y(U, i, copy):
                p = (i - 2) % TILES
                dve.wait_ge(out_proj, U * TILES + i - 1)
                if copy:
                    dve.tensor_copy(y[:, p, :], out_ps[:, :]).then_inc(y_added, 1)
                else:
                    dve.tensor_tensor(out=y[:, p, :], in0=out_ps[:, :], in1=y[:, p, :], op=ALU.add).then_inc(y_added, 1)

            def step(U, i, first, last):
                ahead = not (last and i >= TILES - 1)
                if not (first and i < 2):
                    normalise(U, i)
                if i <= TILES and not (first and i == 0):
                    reciprocal(U, i)
                if ahead:
                    sum_squares(U, tile(U, i + 1), False)
                if not (first and i < 2):
                    add_y(U, i, first)
                if i > TILES:
                    return
                chunks, turns, slots = shape_of_step(i, first)
                for k in range(slots):
                    if k < chunks:
                        bias(U, i, k)
                    if k < turns:
                        low_probs(U, i, k)
                    if ahead and k == min(turns, 3):
                        scale_qk(U, tile(U, i + 1))
                    if ahead and turns and k == turns + 1:
                        low_q(U, (i + 1) % TILES, RING_AT[i] + BEFORE[i] + 1)
                if ahead:
                    r = RING_AT[i] + BEFORE[i] + 1
                    if not turns:
                        low_q(U, i + 1, r)
                    low_k(U, (i + 1) % TILES, r + 1)

            def unit(U, first, last):
                if first:
                    sum_squares(U, tile(U, 0), True)
                    scale_qk(U, tile(U, 0))
                    low_q(U, 0, 0)
                    low_k(U, 0, 1)
                for i in range(TILES + 2 if last else TILES):
                    step(U, i, first, last)

            dve.wait_ge(w_in, 32)
            dve.scalar_tensor_tensor(out=wcol[:, :], in0=norm_w[:, 0:1], scalar=float(P) ** -0.5, in1=norm_w[:, 1:2],
                                     op0=ALU.mult, op1=ALU.mult).then_inc(wcol_done, 1)
            dve.wait_ge(wcol_done, 1)
            dve.wait_ge(consts_in, 32)
            with dve.Fori(0, B) as b:
                dve.wait_ge(x_in, (b + 1) * 16)
                for t in range(TILES):
                    dve.bn_stats(stats[:, t, :], y[:, t, :]).then_inc(stats_done, 1)
                dve.wait_ge(stats_done, (b + 1) * TILES)
                dve.sem_inc(dve_passed, 1)
                for t in range(TILES):
                    dve.bn_aggr(mv[:, t, :], stats[:, t, :]).then_inc(mv_done, 1)
                dve.wait_ge(pool_chain, (b * (UNITS * TILES + 1) + 1) * CHAIN)
                for t in range(TILES):
                    dve.tensor_scalar(y[:, t, :], y[:, t, :], mv[:, t, 0:1], rs_y[:, t:t + 1],
                                      ALU.subtract, ALU.mult).then_inc(xn_done, 1)
                for t in range(TILES):
                    dve.wait_ge(xT_high, b * TILES + t + 1)
                    dve.tensor_tensor(out=xT_lo[:, :, t * P:(t + 1) * P],
                                      in0=ring_ps[:, t % RBANKS, :].rearrange("p (c n) -> p c n", c=DC),
                                      in1=xT_hi[:, :, t * P:(t + 1) * P].bitcast(F32), op=ALU.subtract).then_inc(xT_low, 1)
                dve.memset(y[:, TILES - 2:TILES, :], 0.0).then_inc(y_zero, 1)
                dve.wait_ge(y_zero, b + 1)
                units(dve, b, unit)
                for c in range(CHUNKS):
                    n, k = b * CHUNKS + c, c % 2
                    dve.wait_ge(f_silu_done, n + 1)
                    if c >= 2:
                        dve.wait_ge(f_high, n - 1)
                    dve.tensor_tensor(out=f_prod[k], in0=up_ps[k], in1=f_silu[k], op=ALU.mult).then_inc(f_prod_done, 1)
                    dve.wait_ge(f_high, n + 1)
                    dve.tensor_tensor(out=pT_lo[:, k, :], in0=f_prod[k], in1=pT_hi[:, k, :].bitcast(F32),
                                      op=ALU.subtract).then_inc(f_low, 1)
                    if c in (FC, CHUNKS - 1):
                        if c == FC:
                            dve.wait_ge(x_again_in, (b + 1) * 16)
                        for t in range(HT):
                            m = (0 if c == FC else HT) + t
                            dve.wait_ge(gate_done, b * TILES + m + 1)
                            dve.tensor_tensor(out=y[:, m, :], in0=y[:, m, :], in1=f_gate[m % 2], op=ALU.mult).then_inc(gated, 1)
                            dve.wait_ge(gated, b * TILES + m + 1)
                            dve.tensor_tensor(out=y[:, m, :], in0=y[:, m, :], in1=x_again[:, m, :], op=ALU.add).then_inc(out_ready, 1)

        @block.gpsimd
        def _(pool):
            def chained(ins, done, count):
                ins.then_inc(pool_chain, 1)
                pool.wait_ge(pool_chain, done + count)
                pool.sem_inc(pool_passed, 1)

            def rsqrt(src, n, mul, add, done):
                xx, aa, yy = rs_x[:, 0:n], rs_a[:, 0:n], rs_y[:, 0:n]
                chained(pool.tensor_scalar(xx, src, mul, add, ALU.mult, ALU.add), done, 1)
                chained(pool.tensor_scalar(yy.bitcast(I32), xx.bitcast(I32), -0.5, RSQRT_SEED, ALU.mult, ALU.add), done, 2)
                for k in range(NEWTON):
                    chained(pool.tensor_tensor(out=aa, in0=yy, in1=yy, op=ALU.mult), done, 4 * k + 3)
                    chained(pool.tensor_tensor(out=aa, in0=aa, in1=xx, op=ALU.mult), done, 4 * k + 4)
                    chained(pool.tensor_scalar(aa, aa, -0.5, 1.5, ALU.mult, ALU.add), done, 4 * k + 5)
                    chained(pool.tensor_tensor(out=yy, in0=aa, in1=yy, op=ALU.mult), done, 4 * k + 6)

            def split(hi, lo, src, high, high_count, done):
                pool.sem_inc(pool_passed, 1)
                pool.tensor_copy(hi, src).then_inc(high, 1)
                pool.wait_ge(high, high_count)
                pool.tensor_tensor(out=lo, in0=src, in1=hi.bitcast(F32), op=ALU.subtract).then_inc(done, 1)

            def split_weights(U):
                pool.wait_ge(qkv_in, (U + 1) * 16)
                split(qkv_hi[:, :], qkv_lo[:, :], qkv_raw[:, :], w_high, U + 1, w_split)

            def low_o(U):
                pool.wait_ge(o_high, U + 1)
                pool.tensor_tensor(out=o_lo[:, :, :].rearrange("p g n -> p (g n)"), in0=o_raw[:, :],
                                   in1=o_hi[:, :, :].rearrange("p g n -> p (g n)").bitcast(F32), op=ALU.subtract).then_inc(o_split, 1)

            with pool.Fori(0, B) as b:
                def norms(U, i):
                    t = tile(U, i)
                    if i % TILES == 0:
                        pool.wait_ge(inv_in, (U + 1 + i // TILES) * 16)
                    pool.wait_ge(summed, t)
                    pool.sem_inc(pool_passed, 1)
                    rsqrt(sq_sum[:, 0:G + 1], G + 1, 1.0 / P, RMS_EPS, (b + t) * CHAIN)
                    pool.tensor_tensor(out=rq[:, 0:G + 1], in0=rs_y[:, 0:G + 1], in1=inv_slope[:, :], op=ALU.mult).then_inc(rq_done, 1)

                def split_v(U, i, first):
                    if i == 0 and not first:
                        pool.wait_ge(weighed, U * TURNS)
                    pool.wait_ge(v_staged, tile(U, i))
                    split(v_hi[:, i, :], v_lo[:, i, :], v_nat[:, i % 2, :], v_high, tile(U, i), v_split)

                def low_att(U, i):
                    pool.wait_ge(att_high, U * TILES + i - 1)
                    pool.tensor_tensor(out=attT_lo[:, :, :].rearrange("p g n -> p (g n)"), in0=attT[:, :],
                                       in1=attT_hi[:, :, :].rearrange("p g n -> p (g n)").bitcast(F32), op=ALU.subtract).then_inc(att_split, 1)

                def step(U, i, first, last):
                    if not (first and i < 2):
                        low_att(U, i)
                    if not (last and i >= TILES - 1):
                        norms(U, i + 1)
                    if i < TILES:
                        split_v(U, i, first)
                    if i == 1 and not first:
                        low_o(U)
                    if i == TILES - 2 and not last:
                        pool.wait_ge(projected, tile(U, TILES - 1))
                        split_weights(U + 1)

                def unit(U, first, last):
                    if first:
                        norms(U, 0)
                    for i in range(TILES + 2 if last else TILES):
                        step(U, i, first, last)

                pool.wait_ge(mv_done, (b + 1) * TILES)
                pool.sem_inc(pool_passed, 1)
                rsqrt(mv[:, :, 1], TILES, 1.0, LN_EPS, b * (UNITS * TILES + 1) * CHAIN)
                split_weights(b * UNITS)
                low_o(b * UNITS)
                units(pool, b, unit)

                def split_gate_up(c):
                    n, k = b * CHUNKS + c, c % 2
                    if c < 2:
                        pool.wait_ge(projected, (b + 1) * UNITS * TILES)
                    else:
                        pool.wait_ge(f_gu_done, n - 1)
                    pool.wait_ge(f_in[k], (b * (CHUNKS // 2) + c // 2 + 1) * 16)
                    split(f_hi[k][:, 0:NGU], f_lo[k][:, 0:NGU], f_raw[k][:, 0:NGU], f_gu_high, n + 1, f_gu_split)

                def split_down(c):
                    n, k = b * CHUNKS + c, c % 2
                    if c >= 2:
                        pool.wait_ge(f_down, n - 1)
                    split(f_hi[k][:, NGU:NCH], f_lo[k][:, NGU:NCH], f_raw[k][:, NGU:NCH], f_d_high, n + 1, f_d_split)

                for c in range(CHUNKS):
                    split_gate_up(c)
                    if c:
                        split_down(c - 1)
                split_down(CHUNKS - 1)


_INS = ["x", "w_qkv", "w_o", "w_ffn", "q_norm", "k_norm", "rel", "slopes", "inv_slopes", "ident"]


def kernel(L0_attn_x, L0_attn_Wq, L0_attn_Wk, L0_attn_Wv, L0_attn_Wo, L0_attn_q_norm_w, L0_attn_k_norm_w,
           L0_ffn_w_gate, L0_ffn_w_up, L0_ffn_w_down):
    import concourse.bacc as bacc
    from concourse.bass_utils import run_bass_kernel_spmd

    def by_chunk(w, parts, n):
        return np.asarray(w).reshape(parts, n, DC, P).transpose(0, 3, 2, 1).reshape(parts, P, DC * n)

    def padded(w):
        full = np.zeros((FC * P, D), np.float32)
        full[:INNER] = np.asarray(w)
        return full

    wq = by_chunk(L0_attn_Wq, HKV, G * P)
    wkv = by_chunk(np.concatenate([np.asarray(L0_attn_Wk).reshape(HKV, P, D), np.asarray(L0_attn_Wv).reshape(HKV, P, D)], 1), HKV, KV)
    ffn = np.concatenate([by_chunk(padded(L0_ffn_w_gate), FC, P), by_chunk(padded(L0_ffn_w_up), FC, P),
                          padded(np.asarray(L0_ffn_w_down).T).reshape(FC, P, D)], 2)
    p, u = np.arange(P)[:, None], np.arange(S)[None, :] - (S - P)
    start = 2.0 ** (-2.0 ** -(np.log2(H) - 3))
    slope = np.array([start * start ** i for i in range(H)], np.float32).reshape(HKV, 1, G)
    arrays = {
        "x": np.asarray(L0_attn_x),
        "w_qkv": np.concatenate([wq, wkv], 2),
        "w_o": np.asarray(L0_attn_Wo).T.reshape(HKV, G, P, D).transpose(0, 2, 1, 3).reshape(HKV, P, G * D),
        "w_ffn": ffn,
        "q_norm": np.asarray(L0_attn_q_norm_w).reshape(P, 1),
        "k_norm": np.asarray(L0_attn_k_norm_w).reshape(P, 1),
        "rel": np.where(u <= p, u - p, -MASK).astype(np.float32),
        "slopes": np.broadcast_to(-slope, (HKV, P, G)),
        "inv_slopes": np.broadcast_to(np.concatenate([1 / slope, np.ones((HKV, 1, 1), np.float32)], 2), (HKV, P, G + 1)),
        "ident": np.eye(P, dtype=np.float32),
    }
    nc = bacc.Bacc("TRN2", target_bir_lowering=False, num_devices=1)
    args, feed = [], {}
    for name in _INS:
        a = np.ascontiguousarray(arrays[name])
        feed[f"{name}_dram"] = a
        args.append(nc.dram_tensor(f"{name}_dram", a.shape, mybir.dt.from_np(a.dtype), kind="ExternalInput").ap())
    out = nc.dram_tensor("out_dram", (B, S, D), F32, kind="ExternalOutput").ap()
    build(nc, *args, out)
    got = run_bass_kernel_spmd(nc, [feed], core_ids=[0])
    return got.results[0]["out_dram"]
```

```python
from contextlib import ExitStack

import numpy as np

import concourse.bass as bass
from concourse import mybir

F32 = mybir.dt.float32
F32R = mybir.dt.float32r
I32 = mybir.dt.int32
ALU = mybir.AluOpType
ACT = mybir.ActivationFunctionType
AX = mybir.AxisListType

P = 128
B, S, D = 2, 1024, 512
TILES = S // P
DC = D // P
H, HKV = 32, 8
G = H // HKV
UNITS = HKV
INNER = 1376
FC = -(-INNER // P)
HALVES = 2
CHUNKS = HALVES * FC
CHAINS = UNITS * TILES + 1
HT = TILES // HALVES
BANK = 512
KV = 2 * P
NW = D + KV
NGU = 2 * DC * P
NCH = NGU + D
NQK = (G + 1) * P
VBUFS = 4
MASK = 2.0 ** 110
LN_EPS, RMS_EPS = 1e-5, 1e-6
RSQRT_SEED = float(0x5F3759DF)
NEWTON = 3
CHAIN = 2 + 4 * NEWTON

HEAD_CHUNKS = [-(-(i + 1) * P // BANK) for i in range(TILES)]
SCORE_AT = [G * sum(HEAD_CHUNKS[:i]) for i in range(TILES + 1)]
SCORES = SCORE_AT[TILES]
TURNS = TILES * (TILES + 1) // 2
BEFORE = [TILES] + list(range(1, TILES))
TURN_AT = [sum(BEFORE[1:i + 1]) - BEFORE[i] for i in range(TILES)] + [TURNS - TILES]
RING, LOWS = TURNS + 3 * TILES, TURNS + 2 * TILES
RING_AT, LOW_AT = [3 - 2 - TILES], [2 - TILES]
for _i in range(TILES):
    RING_AT.append(RING_AT[-1] + BEFORE[_i] + 3)
    LOW_AT.append(LOW_AT[-1] + BEFORE[_i] + 2)
STEADY_LOW = list(LOW_AT)
RING_AT[TILES] -= 2
LOW_AT[TILES] -= 2
RBANKS = 3
SLOTS = 4
LAG = 2


def ring_low(r, first, ending):
    if first and r < 2:
        return r
    if ending and r >= RING_AT[TILES]:
        j = r - RING_AT[TILES]
        return LOW_AT[TILES] + j if j < TILES else None
    if r < RING_AT[0]:
        low = ring_low(r + RING, False, False)
        return None if low is None else low - LOWS
    i = max(k for k in range(TILES) if RING_AT[k] <= r)
    j = r - RING_AT[i]
    if j == BEFORE[i]:
        return None
    return LOW_AT[i] + j - (j > BEFORE[i])


def shape_of_step(i, first):
    chunks = G * HEAD_CHUNKS[i] if i < TILES else 0
    turns = 0 if first and i == 0 else TILES if i == TILES else BEFORE[i]
    return chunks, turns, max(chunks, turns + LAG if turns else 0)


def build(nc, x, w_qkv, w_o, w_ffn, q_norm, k_norm, rel, slopes, inv_slopes, ident_in, out):
    ctx = ExitStack()
    with ctx:
        def sb(name, shape, dt=F32):
            return ctx.enter_context(nc.sbuf_tensor(name, shape, dt))

        def psum(name, shape):
            return ctx.enter_context(nc.psum_tensor(name, shape, F32))

        def sem(name):
            return ctx.enter_context(nc.semaphore(name))

        xT_hi, xT_lo = sb("xT_hi", [P, DC, S], F32R), sb("xT_lo", [P, DC, S], F32R)
        y = sb("y", [P, TILES, D])
        qkv_raw, o_raw = sb("qkv_raw", [P, DC, NW]), sb("o_raw", [P, G * D])
        qkv_hi, qkv_lo = sb("qkv_hi", [P, DC, NW], F32R), sb("qkv_lo", [P, DC, NW], F32R)
        o_hi, o_lo = sb("o_hi", [P, G * D], F32R), sb("o_lo", [P, G * D], F32R)
        kv_hi, kv_lo = sb("kv_hi", [P, 2 * S], F32R), sb("kv_lo", [P, 2 * S], F32R)
        kT_hi, kT_lo = kv_hi[:, 0:S], kv_lo[:, 0:S]
        v_hi, v_lo = kv_hi[:, S:2 * S], kv_lo[:, S:2 * S]
        qT_hi, qT_lo = sb("qT_hi", [P, 2, G * P], F32R), sb("qT_lo", [P, 2, G * P], F32R)
        probs = [sb("probs0", [P, G, S - P]), sb("probs1", [P, G, S])]
        pT_hi, pT_lo = sb("pT_hi", [P, SLOTS, G * P], F32R), sb("pT_lo", [P, SLOTS, G * P], F32R)
        attT, recT = sb("attT", [P, G * P]), sb("recT", [P, G * P])
        attT_hi, attT_lo = sb("attT_hi", [P, G * P], F32R), sb("attT_lo", [P, G * P], F32R)
        natural = sb("natural", [P, 3 * NQK])
        qk = [natural[:, k * NQK:(k + 1) * NQK] for k in range(2)]
        qk_sq = natural[:, 2 * NQK:3 * NQK]
        v_nat = sb("v_nat", [P, VBUFS, P])
        rel_sb, ident = sb("rel_sb", [P, S]), sb("ident", [P, P])
        slope, inv_slope = sb("slope", [P, G]), sb("inv_slope", [P, G + 1])
        norm_w, wcol = sb("norm_w", [P, 2]), sb("wcol", [P, 1])
        low_min = sb("low_min", [P, 2, G, 2])
        row_sum, rec = sb("row_sum", [P, 2, G]), sb("rec", [P, G])
        sq_sum, rq = sb("sq_sum", [P, G + 1]), sb("rq", [P, G + 1])
        rs_x, rs_a, rs_y = sb("rs_x", [P, TILES]), sb("rs_a", [P, TILES]), sb("rs_y", [P, TILES])
        stats, mv = sb("stats", [P, TILES, 6]), sb("mv", [P, TILES, 2])

        f_raw = [natural[:, 0:NCH], o_raw[:, 0:NCH]]
        f_hi, f_lo = [kv_hi[:, 0:NCH], o_hi[:, 0:NCH]], [kv_lo[:, 0:NCH], o_lo[:, 0:NCH]]
        probs0 = probs[0][:, :, :].rearrange("p g n -> p (g n)")
        f_silu = [probs0[:, k * BANK:(k + 1) * BANK] for k in range(2)]
        f_prod = [probs0[:, (2 + k) * BANK:(3 + k) * BANK] for k in range(2)]
        f_gate = [probs0[:, (4 + k) * BANK:(5 + k) * BANK] for k in range(2)]
        x_again = [attT, recT]
        xn = probs[1][:, :, :].rearrange("p g n -> p (g n)").rearrange("p (t d) -> p t d", d=D)

        qkv_ps = psum("qkv_ps", [P, 2 * BANK])
        score_ps = psum("score_ps", [P, 2, BANK])
        ring_ps = psum("ring_ps", [P, RBANKS, BANK])
        out_ps = psum("out_ps", [P, BANK])
        gate_ps = [score_ps[:, k, :] for k in range(2)]
        up_ps = [qkv_ps[:, k * BANK:(k + 1) * BANK] for k in range(2)]
        xT_ps = [score_ps[:, 0, :], score_ps[:, 1, :], qkv_ps[:, 0:BANK], qkv_ps[:, BANK:2 * BANK]]
        down_ps = [ring_ps[:, k, :] for k in range(RBANKS)] + [out_ps[:, :]]
        assert HT == len(down_ps)

        consts_in, w_in = sem("consts_in"), sem("w_in")
        x_in = [sem("x_in0"), sem("x_in1")]
        x_again_in = [sem("x_again_in0"), sem("x_again_in1")]
        qkv_in, o_in, slope_in, inv_in = sem("qkv_in"), sem("o_in"), sem("slope_in"), sem("inv_in")
        f_in = [sem("f_in0"), sem("f_in1")]
        stats_done, mv_done = sem("stats_done"), sem("mv_done")
        xn_done, xT_turned, xT_high, xT_low = sem("xn_done"), sem("xT_turned"), sem("xT_high"), sem("xT_low")
        y_free, y_zero = sem("y_free"), sem("y_zero")
        w_high, w_split, o_high, o_split = sem("w_high"), sem("w_split"), sem("o_high"), sem("o_split")
        projected, squared, summed, rq_done = sem("projected"), sem("squared"), sem("summed"), sem("rq_done")
        qk_done, v_staged, v_high, v_split = sem("qk_done"), sem("v_staged"), sem("v_high"), sem("v_split")
        scored, biased, exped = sem("scored"), sem("biased"), sem("exped")
        ring_full, ring_high, ring_lowd = sem("ring_full"), sem("ring_high"), sem("ring_lowd")
        weighed, rec_done = sem("weighed"), sem("rec_done")
        att_done, att_high, att_split = sem("att_done"), sem("att_high"), sem("att_split")
        out_proj, y_added = sem("out_proj"), sem("y_added")
        pool_chain = sem("pool_chain")
        f_gu_high, f_d_high = sem("f_gu_high"), sem("f_d_high")
        f_gu_split, f_d_split = sem("f_gu_split"), sem("f_d_split")
        f_gu_done, f_silu_done, f_prod_done = sem("f_gu_done"), sem("f_silu_done"), sem("f_prod_done")
        f_high, f_low, f_down = sem("f_high"), sem("f_low"), sem("f_down")
        gate_done, gated, out_ready, stored = sem("gate_done"), sem("gated"), sem("out_ready"), sem("stored")
        sp_passed, dve_passed, pool_passed, wcol_done = sem("sp_passed"), sem("dve_passed"), sem("pool_passed"), sem("wcol_done")

        block = ctx.enter_context(nc.Block())

        def units(eng, b, body):
            body(b * UNITS, True, False)
            with eng.Fori(1, UNITS - 1) as g:
                body(b * UNITS + g, False, False)
            body(b * UNITS + UNITS - 1, False, True)

        def tile(U, i):
            return U * TILES + i + 1

        @block.sync
        def _(sp):
            def alone(sem, value):
                sp.wait_ge(sem, value)
                sp.sem_inc(sp_passed, 1)

            def load_unit(g):
                sp.dma_start(qkv_raw[:, :, :].rearrange("p c n -> p (c n)"),
                             w_qkv[bass.ds(g, 1), :, :].rearrange("a p n -> p (a n)")).then_inc(qkv_in, 16)

            def load_o(g):
                sp.dma_start(o_raw[:, :], w_o[bass.ds(g, 1), :, :].rearrange("a p n -> p (a n)")).then_inc(o_in, 16)

            def load_inv(g):
                sp.dma_start(inv_slope[:, :], inv_slopes[bass.ds(g, 1), :, :].rearrange("a p n -> p (a n)")).then_inc(inv_in, 16)

            def load_slope(g):
                sp.dma_start(slope[:, :], slopes[bass.ds(g, 1), :, :].rearrange("a p n -> p (a n)")).then_inc(slope_in, 16)

            def load_x(row):
                for half in range(HALVES):
                    sp.dma_start(xn[:, half * HT:(half + 1) * HT, :],
                                 x[bass.ds(row, 1), half * BANK:(half + 1) * BANK, :].rearrange("a (t p) d -> p (a t) d", p=P)
                                 ).then_inc(x_in[half], 16)

            load_x(0)
            sp.dma_start(ident[:, :], ident_in).then_inc(consts_in, 16)
            load_unit(0)
            sp.dma_start(norm_w[:, 0:1], q_norm).then_inc(w_in, 16)
            sp.dma_start(norm_w[:, 1:2], k_norm).then_inc(w_in, 16)
            load_inv(0)
            sp.dma_start(rel_sb[:, :], rel).then_inc(consts_in, 16)
            load_slope(0)
            load_o(0)
            sp.sem_inc(y_free, 1)

            with sp.Fori(0, B) as b:
                def unit_loads(U, after):
                    alone(w_split, (U + 1) * DC)
                    load_unit(after)
                    if not isinstance(after, int):
                        alone(o_split, U + 1)
                        load_o(after)
                    alone(rq_done, (U + 1) * TILES)
                    load_inv(after)
                    alone(biased, (U + 1) * SCORES)
                    load_slope(after)

                with sp.Fori(0, UNITS - 1) as g:
                    unit_loads(b * UNITS + g, g + 1)
                unit_loads(b * UNITS + UNITS - 1, 0)

                def load_x_again(m):
                    sp.dma_start(x_again[m % 2][:, :], x[bass.ds(b, 1), m * P:(m + 1) * P, :].rearrange("a p d -> p (a d)")
                                 ).then_inc(x_again_in[m % 2], 16)

                def store(m):
                    alone(out_ready, b * TILES + m + 1)
                    sp.dma_start(out[bass.ds(b, 1), m * P:(m + 1) * P, :].rearrange("a p d -> p (a d)"),
                                 y[:, m, :]).then_inc(stored, 16)
                    if m + 2 < TILES:
                        load_x_again(m + 2)

                alone(y_added, (b + 1) * UNITS * TILES)
                for c in range(CHUNKS):
                    if c >= 2:
                        alone(f_d_split, b * CHUNKS + c - 1)
                    sp.dma_start(f_raw[c % 2], w_ffn[c % FC]).then_inc(f_in[c % 2], 16)
                    if c == 2:
                        load_x_again(0)
                        load_x_again(1)
                        load_x(B - 1)
                    if c == FC + 2:
                        for m in range(HT):
                            store(m)
                alone(f_d_split, (b + 1) * CHUNKS)
                load_o(0)
                for m in range(HT, TILES):
                    store(m)
                alone(stored, (b + 1) * TILES * 16)
                sp.sem_inc(y_free, 1)
            sp.wait_ge(o_in, (B * UNITS + 1) * 16)

        @block.tensor
        def _(pe):
            def ring_free(U, r, first, ending):
                q = r - RBANKS
                if first and q < 0:
                    return
                low = ring_low(q, first, ending)
                if low is None:
                    pe.wait_ge(ring_high, U * RING + q + 1)
                else:
                    pe.wait_ge(ring_lowd, U * LOWS + low + 1)

            def project(U, i, first):
                if not first:
                    pe.wait_ge(qk_done, tile(U, i) - 1)
                    pe.wait_ge(v_staged, tile(U, i) - 1)
                for c in range(DC):
                    if i == 0:
                        pe.wait_ge(w_split, U * DC + c + 1)
                    for xT, w in ((xT_hi, qkv_hi), (xT_hi, qkv_lo), (xT_lo, qkv_hi)):
                        a = xT[:, c, i * P:(i + 1) * P]
                        go, end = c == 0 and xT is xT_hi and w is qkv_hi, c == DC - 1 and xT is xT_lo
                        pe.matmul(qkv_ps[:, 0:BANK], a, w[:, c, 0:D], start=go, stop=end)
                        mm = pe.matmul(qkv_ps[:, BANK:BANK + KV], a, w[:, c, D:NW], start=go, stop=end)
                mm.then_inc(projected, 1)

            def turn_q(U, i, r, first, ending, t):
                ring_free(U, r, first, ending)
                pe.wait_ge(qk_done, t)
                for h in range(G):
                    tr = pe.transpose(ring_ps[:, r % RBANKS, h * P:(h + 1) * P], qk[i % 2][:, h * P:(h + 1) * P], ident[:, :])
                tr.then_inc(ring_full, 1)

            def turn_k(U, i, r, first, ending):
                ring_free(U, r, first, ending)
                pe.transpose(ring_ps[:, r % RBANKS, 0:P], qk[i % 2][:, G * P:NQK], ident[:, :]).then_inc(ring_full, 1)

            def scores(U, i, k, first):
                n = SCORE_AT[i] + k
                h, part = k // HEAD_CHUNKS[i], k % HEAD_CHUNKS[i]
                lo, hi = part * BANK, min((part + 1) * BANK, (i + 1) * P)
                if k == 0:
                    low = 1 if first and i == 0 else STEADY_LOW[i] - 1
                    pe.wait_ge(ring_lowd, U * LOWS + low + 1)
                if not (first and n < 2):
                    pe.wait_ge(biased, U * SCORES + n - 1)
                for q, kt in ((qT_hi, kT_hi), (qT_hi, kT_lo), (qT_lo, kT_hi)):
                    mm = pe.matmul(score_ps[:, n % 2, 0:hi - lo], q[:, i % 2, h * P:(h + 1) * P], kt[:, lo:hi],
                                   start=(q is qT_hi and kt is kT_hi), stop=(q is qT_lo))
                mm.then_inc(scored, 1)

            def turn_probs(U, i, j, first, ending):
                r, p = RING_AT[i] + j, (i - 1) % TILES
                ring_free(U, r, first, ending)
                for h in range(G):
                    if j == 0:
                        pe.wait_ge(exped, (U * TILES + i - 1) * G + h + 1)
                    tr = pe.transpose(ring_ps[:, r % RBANKS, h * P:(h + 1) * P],
                                      probs[p % 2][:, h, j * P:(j + 1) * P], ident[:, :])
                tr.then_inc(ring_full, 1)

            def turn_rec(U, i, turns, first, ending):
                r = RING_AT[i] + turns
                ring_free(U, r, first, ending)
                pe.wait_ge(rec_done, U * TILES + i)
                for h in range(G):
                    tr = pe.transpose(ring_ps[:, r % RBANKS, h * P:(h + 1) * P],
                                      rec[:, h:h + 1].to_broadcast([P, P]), ident[:, :])
                tr.then_inc(ring_full, 1)

            def weigh(U, i, j, turns, first):
                if j == 0:
                    pe.wait_ge(v_split, U * TILES + i)
                    if not (first and i < 2):
                        pe.wait_ge(y_added, U * TILES + i - 1)
                pe.wait_ge(ring_lowd, U * LOWS + LOW_AT[i] + j + 1)
                slot = (TURN_AT[i] + j) % SLOTS
                for v, pt in ((v_hi, pT_hi), (v_hi, pT_lo), (v_lo, pT_hi)):
                    mm = pe.matmul(out_ps[:, :], v[:, j * P:(j + 1) * P], pt[:, slot, :],
                                   start=(j == 0 and v is v_hi and pt is pT_hi),
                                   stop=(j == turns - 1 and v is v_lo))
                mm.then_inc(weighed, 1)

            def out_project(U, i, wait_w):
                if wait_w:
                    pe.wait_ge(o_split, U + 1)
                pe.wait_ge(att_split, U * TILES + i - 1)
                for h in range(G):
                    for a, w in ((attT_hi, o_hi), (attT_hi, o_lo), (attT_lo, o_hi)):
                        mm = pe.matmul(out_ps[:, :], a[:, h * P:(h + 1) * P], w[:, h * D:(h + 1) * D],
                                       start=(h == 0 and a is attT_hi and w is o_hi),
                                       stop=(h == G - 1 and a is attT_lo))
                mm.then_inc(out_proj, 1)

            def step(U, i, first, last):
                ending = i >= TILES
                ahead = not (last and i >= TILES - 1)
                if not (last and i >= TILES - 2):
                    project(U + (i + 2) // TILES, (i + 2) % TILES, False)
                if not (first and i < 2):
                    out_project(U, i, i == 2)
                if i > TILES:
                    return
                chunks, turns, slots = shape_of_step(i, first)
                for k in range(slots):
                    if k < chunks:
                        scores(U, i, k, first)
                    if k < turns:
                        turn_probs(U, i, k, first, ending)
                    if turns and k == turns:
                        turn_rec(U, i, turns, first, ending)
                    if ahead and turns and k == turns + 1:
                        turn_q(U, (i + 1) % TILES, RING_AT[i] + BEFORE[i] + 1, first, ending, tile(U, i + 1))
                        turn_k(U, (i + 1) % TILES, RING_AT[i] + BEFORE[i] + 2, first, ending)
                    if 0 <= k - LAG < turns:
                        weigh(U, i, k - LAG, turns, first)
                if not turns:
                    turn_q(U, i + 1, RING_AT[i] + BEFORE[i] + 1, first, ending, tile(U, i + 1))
                    turn_k(U, i + 1, RING_AT[i] + BEFORE[i] + 2, first, ending)

            def unit(U, first, last):
                if first:
                    project(U, 0, True)
                    project(U, 1, False)
                    turn_q(U, 0, 0, True, False, tile(U, 0))
                    turn_k(U, 0, 1, True, False)
                for i in range(TILES + 2 if last else TILES):
                    step(U, i, first, last)

            pe.wait_ge(consts_in, 32)
            with pe.Fori(0, B) as b:
                for t in range(TILES):
                    pe.wait_ge(xn_done, b * TILES + t + 1)
                    if t >= len(xT_ps):
                        pe.wait_ge(xT_low, b * TILES + t - len(xT_ps) + 1)
                    for c in range(DC):
                        tr = pe.transpose(xT_ps[t % len(xT_ps)][:, c * P:(c + 1) * P], xn[:, t, c * P:(c + 1) * P], ident[:, :])
                    tr.then_inc(xT_turned, 1)
                pe.wait_ge(xT_low, (b + 1) * TILES)
                units(pe, b, unit)

                def gate_up(c):
                    n, k, half = b * CHUNKS + c, c % 2, c // FC
                    pe.wait_ge(f_gu_split, n + 1)
                    if c >= 2:
                        pe.wait_ge(f_prod_done, n - 1)
                    for part, acc in ((0, gate_ps[k]), (1, up_ps[k])):
                        for d in range(DC):
                            for w, xT in ((f_hi, xT_hi), (f_hi, xT_lo), (f_lo, xT_hi)):
                                at = (part * DC + d) * P
                                mm = pe.matmul(acc, w[k][:, at:at + P], xT[:, d, half * BANK:(half + 1) * BANK],
                                               start=(d == 0 and w is f_hi and xT is xT_hi),
                                               stop=(d == DC - 1 and w is f_lo))
                    mm.then_inc(f_gu_done, 1)

                def down(c):
                    n, k = b * CHUNKS + c, c % 2
                    pe.wait_ge(f_d_split, n + 1)
                    pe.wait_ge(f_low, n + 1)
                    if c == 0:
                        pe.wait_ge(y_added, (b + 1) * UNITS * TILES)
                    if c == FC:
                        pe.wait_ge(gate_done, b * TILES + HT)
                    for t in range(HT):
                        for a, w in ((pT_hi, f_hi), (pT_hi, f_lo), (pT_lo, f_hi)):
                            mm = pe.matmul(down_ps[t], a[:, k, t * P:(t + 1) * P], w[k][:, NGU:NCH],
                                           start=(c % FC == 0 and a is pT_hi and w is f_hi),
                                           stop=(c % FC == FC - 1 and a is pT_lo))
                    mm.then_inc(f_down, 1)

                for c in range(CHUNKS):
                    gate_up(c)
                    if c:
                        down(c - 1)
                down(CHUNKS - 1)

        @block.scalar
        def _(act):
            def square(t, first):
                act.wait_ge(projected, t)
                if not first:
                    act.wait_ge(summed, t - 1)
                act.activation(qk_sq, qkv_ps[:, 0:(G + 1) * P], ACT.Square).then_inc(squared, 1)

            def stage_v(i, t, early):
                if not early:
                    act.wait_ge(v_split, t - VBUFS)
                act.activation(v_nat[:, i % VBUFS, :], qkv_ps[:, BANK + P:BANK + KV], ACT.Copy).then_inc(v_staged, 1)

            def high_q(U, i, r):
                act.wait_ge(ring_full, U * RING + r + 1)
                act.activation(qT_hi[:, i % 2, :], ring_ps[:, r % RBANKS, :],
                               ACT.Copy, scale=wcol[:, 0:1]).then_inc(ring_high, 1)

            def high_k(U, i, r):
                act.wait_ge(ring_full, U * RING + r + 1)
                act.activation(kT_hi[:, i * P:(i + 1) * P], ring_ps[:, r % RBANKS, 0:P], ACT.Copy).then_inc(ring_high, 1)

            def exp(U, i, h):
                act.wait_ge(biased, U * SCORES + SCORE_AT[i] + (h + 1) * HEAD_CHUNKS[i])
                row = probs[i % 2][:, h, 0:(i + 1) * P]
                act.activation(row, row, ACT.Exp, scale=-1.0, bias=low_min[:, i % 2, h, HEAD_CHUNKS[i] - 1:HEAD_CHUNKS[i]],
                               accum_out=row_sum[:, i % 2, h:h + 1]).then_inc(exped, 1)

            def high_probs(U, i, j, first):
                r, n = RING_AT[i] + j, TURN_AT[i] + j
                act.wait_ge(ring_full, U * RING + r + 1)
                if not (first and n < SLOTS):
                    act.wait_ge(weighed, U * TURNS + n - SLOTS + 1)
                act.activation(pT_hi[:, n % SLOTS, :], ring_ps[:, r % RBANKS, :], ACT.Copy).then_inc(ring_high, 1)

            def copy_rec(U, i, turns):
                r = RING_AT[i] + turns
                act.wait_ge(ring_full, U * RING + r + 1)
                act.activation(recT[:, :], ring_ps[:, r % RBANKS, :], ACT.Copy).then_inc(ring_high, 1)

            def high_att(U, i):
                act.wait_ge(att_done, U * TILES + i - 1)
                act.activation(attT_hi[:, :], attT[:, :], ACT.Copy).then_inc(att_high, 1)

            def high_o(U, used):
                act.wait_ge(o_in, (U + 1) * 16)
                if used:
                    act.wait_ge(out_proj, U * TILES)
                act.activation(o_hi[:, :], o_raw[:, :], ACT.Copy).then_inc(o_high, 1)

            def high_w(U, c):
                act.activation(qkv_hi[:, c, :], qkv_raw[:, c, :], ACT.Copy).then_inc(w_high, 1)

            def step(U, i, first, last):
                ahead = not (last and i >= TILES - 1)
                if not (first and i < 2):
                    high_att(U, i)
                if i > TILES:
                    return
                if not (last and i >= TILES - 2):
                    square(tile(U, i + 2), False)
                    stage_v((i + 2) % TILES, tile(U, i + 2), first and i < 2)
                chunks, turns, slots = shape_of_step(i, first)
                for k in range(slots + 1):
                    if k < turns:
                        high_probs(U, i, k, first)
                    if turns and k == turns:
                        copy_rec(U, i, turns)
                    if ahead and turns and k == turns + 1:
                        high_q(U, (i + 1) % TILES, RING_AT[i] + BEFORE[i] + 1)
                        high_k(U, (i + 1) % TILES, RING_AT[i] + BEFORE[i] + 2)
                    if 1 <= k <= chunks and k % HEAD_CHUNKS[i] == 0:
                        exp(U, i, k // HEAD_CHUNKS[i] - 1)
                    if k == 1 and i == 1 and not first:
                        high_o(U, True)
                    if i == TILES - 3 and k < DC:
                        if k == 0:
                            act.wait_ge(qkv_in, (U + 2) * 16)
                            act.wait_ge(projected, tile(U, TILES - 1))
                        high_w(U + 1, k)
                if not turns:
                    high_q(U, i + 1, RING_AT[i] + BEFORE[i] + 1)
                    high_k(U, i + 1, RING_AT[i] + BEFORE[i] + 2)

            def unit(U, first, last):
                if first:
                    square(tile(U, 0), True)
                    stage_v(0, tile(U, 0), True)
                    square(tile(U, 1), False)
                    stage_v(1, tile(U, 1), True)
                    high_q(U, 0, 0)
                    high_k(U, 0, 1)
                    high_o(U, False)
                for i in range(TILES + 2 if last else TILES):
                    step(U, i, first, last)

            act.wait_ge(wcol_done, 1)
            act.wait_ge(qkv_in, 16)
            for c in range(DC):
                high_w(0, c)
            with act.Fori(0, B) as b:
                for t in range(TILES):
                    act.wait_ge(xT_turned, b * TILES + t + 1)
                    act.activation(xT_hi[:, :, t * P:(t + 1) * P],
                                   xT_ps[t % len(xT_ps)].rearrange("p (c n) -> p c n", c=DC), ACT.Copy).then_inc(xT_high, 1)
                units(act, b, unit)

                def high_gate_up(c):
                    n, k = b * CHUNKS + c, c % 2
                    act.wait_ge(f_in[k], (b * (CHUNKS // 2) + c // 2 + 1) * 16)
                    if c >= 2:
                        act.wait_ge(f_gu_done, n - 1)
                    act.activation(f_hi[k][:, 0:NGU], f_raw[k][:, 0:NGU], ACT.Copy).then_inc(f_gu_high, 1)

                def high_down(c):
                    n, k = b * CHUNKS + c, c % 2
                    if c >= 2:
                        act.wait_ge(f_down, n - 1)
                    act.activation(f_hi[k][:, NGU:NCH], f_raw[k][:, NGU:NCH], ACT.Copy).then_inc(f_d_high, 1)

                high_gate_up(0)
                high_gate_up(1)
                high_down(0)
                for c in range(CHUNKS):
                    n, k = b * CHUNKS + c, c % 2
                    act.wait_ge(f_gu_done, n + 1)
                    act.activation(f_silu[k], gate_ps[k], ACT.Silu).then_inc(f_silu_done, 1)
                    if c + 2 < CHUNKS:
                        high_gate_up(c + 2)
                    act.wait_ge(f_prod_done, n + 1)
                    if c >= 2:
                        act.wait_ge(f_down, n - 1)
                    act.activation(pT_hi[:, k, :], f_prod[k], ACT.Copy).then_inc(f_high, 1)
                    if c + 1 < CHUNKS:
                        high_down(c + 1)
                    if c in (FC, CHUNKS - 1):
                        half = 0 if c == FC else 1
                        act.wait_ge(f_down, b * CHUNKS + (half + 1) * FC)
                        for t in range(HT):
                            m = half * HT + t
                            if m >= 2:
                                act.wait_ge(gated, b * TILES + m - 1)
                            act.activation(f_gate[m % 2], down_ps[t], ACT.Silu).then_inc(gate_done, 1)

        @block.vector
        def _(dve):
            def sum_squares(t, first):
                dve.wait_ge(squared, t)
                if not first:
                    dve.wait_ge(rq_done, t - 1)
                dve.tensor_reduce(sq_sum[:, :], qk_sq.rearrange("p (g n) -> p g n", g=G + 1),
                                  AX.X, ALU.add).then_inc(summed, 1)

            def scale_qk(i, t):
                dve.wait_ge(rq_done, t)
                dve.wait_ge(v_staged, t)
                dve.tensor_tensor(out=qk[i % 2].rearrange("p (g n) -> p g n", g=G + 1), in0=qkv_ps[:, 0:(G + 1) * P].rearrange("p (g n) -> p g n", g=G + 1),
                                  in1=rq[:, :].unsqueeze(2).to_broadcast([P, G + 1, P]), op=ALU.mult).then_inc(qk_done, 1)

            def low_q(U, i, r):
                dve.wait_ge(ring_high, U * RING + r + 1)
                dve.scalar_tensor_tensor(out=qT_lo[:, i % 2, :], in0=ring_ps[:, r % RBANKS, :],
                                         scalar=wcol[:, 0:1], in1=qT_hi[:, i % 2, :].bitcast(F32),
                                         op0=ALU.mult, op1=ALU.subtract).then_inc(ring_lowd, 1)

            def low_k(U, i, r):
                dve.wait_ge(ring_high, U * RING + r + 1)
                dve.tensor_tensor(out=kT_lo[:, i * P:(i + 1) * P], in0=ring_ps[:, r % RBANKS, 0:P],
                                  in1=kT_hi[:, i * P:(i + 1) * P].bitcast(F32), op=ALU.subtract).then_inc(ring_lowd, 1)

            def bias(U, i, k):
                n = SCORE_AT[i] + k
                h, part = k // HEAD_CHUNKS[i], k % HEAD_CHUNKS[i]
                lo, hi = part * BANK, min((part + 1) * BANK, (i + 1) * P)
                if k == 0 and i == 0:
                    dve.wait_ge(slope_in, (U + 1) * 16)
                if part:
                    dve.wait_ge(biased, U * SCORES + n)
                dve.wait_ge(scored, U * SCORES + n + 1)
                dve.sem_inc(dve_passed, 1)
                at = S - (i + 1) * P + lo
                dve.tensor_tensor_reduce(
                    out=probs[i % 2][:, h, lo:hi], in0=score_ps[:, n % 2, 0:hi - lo], in1=rel_sb[:, at:at + hi - lo],
                    scale=slope[:, h:h + 1], scalar=low_min[:, i % 2, h, 0:1] if part else 3.0e38,
                    op0=ALU.add, op1=ALU.min, accum_out=low_min[:, i % 2, h, part:part + 1]).then_inc(biased, 1)

            def low_probs(U, i, j):
                r, n = RING_AT[i] + j, TURN_AT[i] + j
                dve.wait_ge(ring_high, U * RING + r + 1)
                dve.tensor_tensor(out=pT_lo[:, n % SLOTS, :], in0=ring_ps[:, r % RBANKS, :],
                                  in1=pT_hi[:, n % SLOTS, :].bitcast(F32), op=ALU.subtract).then_inc(ring_lowd, 1)

            def reciprocal(U, i):
                dve.wait_ge(exped, (U * TILES + i) * G)
                dve.reciprocal(rec[:, :], row_sum[:, (i - 1) % 2, :]).then_inc(rec_done, 1)

            def normalise(U, i):
                dve.wait_ge(weighed, U * TURNS + (TURN_AT[i] if i <= TILES else TURNS))
                r = (RING_AT[TILES - 1] + BEFORE[TILES - 1] - RING if i == 0
                     else RING_AT[TILES] + TILES if i == TILES + 1 else RING_AT[i - 1] + BEFORE[i - 1])
                dve.wait_ge(ring_high, U * RING + r + 1)
                dve.tensor_tensor(out=attT[:, :], in0=out_ps[:, :], in1=recT[:, :], op=ALU.mult).then_inc(att_done, 1)

            def add_y(U, i, copy):
                p = (i - 2) % TILES
                dve.wait_ge(out_proj, U * TILES + i - 1)
                if copy:
                    dve.tensor_copy(y[:, p, :], out_ps[:, :]).then_inc(y_added, 1)
                else:
                    dve.tensor_tensor(out=y[:, p, :], in0=out_ps[:, :], in1=y[:, p, :], op=ALU.add).then_inc(y_added, 1)

            dve.wait_ge(w_in, 32)
            dve.scalar_tensor_tensor(out=wcol[:, :], in0=norm_w[:, 0:1], scalar=float(P) ** -0.5, in1=norm_w[:, 1:2],
                                     op0=ALU.mult, op1=ALU.mult).then_inc(wcol_done, 1)
            dve.wait_ge(wcol_done, 1)
            dve.wait_ge(consts_in, 32)
            def row_stats(row):
                for t in range(TILES):
                    if t % HT == 0:
                        dve.wait_ge(x_in[t // HT], (row + 1) * 16)
                    dve.bn_stats(stats[:, t, :], xn[:, t, :]).then_inc(stats_done, 1)
                dve.wait_ge(stats_done, (row + 1) * TILES)
                dve.sem_inc(dve_passed, 1)
                for t in range(TILES):
                    dve.bn_aggr(mv[:, t, :], stats[:, t, :]).then_inc(mv_done, 1)

            def normalise_x(row):
                dve.wait_ge(pool_chain, (row * CHAINS + 1) * CHAIN)
                for t in range(TILES):
                    dve.tensor_scalar(xn[:, t, :], xn[:, t, :], mv[:, t, 0:1], rs_y[:, t:t + 1],
                                      ALU.subtract, ALU.mult).then_inc(xn_done, 1)

            row_stats(0)
            normalise_x(0)
            with dve.Fori(0, B) as b:
                for t in range(TILES):
                    dve.wait_ge(xT_high, b * TILES + t + 1)
                    dve.tensor_tensor(out=xT_lo[:, :, t * P:(t + 1) * P],
                                      in0=xT_ps[t % len(xT_ps)].rearrange("p (c n) -> p c n", c=DC),
                                      in1=xT_hi[:, :, t * P:(t + 1) * P].bitcast(F32), op=ALU.subtract).then_inc(xT_low, 1)

                def step(U, i, first, last):
                    ahead = not (last and i >= TILES - 1)
                    if not (first and i < 2):
                        normalise(U, i)
                    if i <= TILES and not (first and i == 0):
                        reciprocal(U, i)
                    if not (last and i >= TILES - 2):
                        sum_squares(tile(U, i + 2), False)
                    if not (first and i < 2):
                        if first and i == 2:
                            dve.wait_ge(y_free, b + 1)
                            dve.memset(y[:, TILES - 2:TILES, :], 0.0).then_inc(y_zero, 1)
                            dve.wait_ge(y_zero, b + 1)
                        add_y(U, i, first)
                    if i > TILES:
                        return
                    chunks, turns, slots = shape_of_step(i, first)
                    for k in range(slots):
                        if k < chunks:
                            bias(U, i, k)
                        if k < turns:
                            low_probs(U, i, k)
                        if k == 2 and not (last and i >= TILES - 2):
                            scale_qk((i + 2) % TILES, tile(U, i + 2))
                        if ahead and turns and k == turns + 1:
                            low_q(U, (i + 1) % TILES, RING_AT[i] + BEFORE[i] + 1)
                            low_k(U, (i + 1) % TILES, RING_AT[i] + BEFORE[i] + 2)
                    if not turns:
                        low_q(U, i + 1, RING_AT[i] + BEFORE[i] + 1)
                        low_k(U, i + 1, RING_AT[i] + BEFORE[i] + 2)

                def unit(U, first, last):
                    if first:
                        sum_squares(tile(U, 0), True)
                        scale_qk(0, tile(U, 0))
                        sum_squares(tile(U, 1), False)
                        scale_qk(1, tile(U, 1))
                        low_q(U, 0, 0)
                        low_k(U, 0, 1)
                    for i in range(TILES + 2 if last else TILES):
                        step(U, i, first, last)

                units(dve, b, unit)
                for c in range(CHUNKS):
                    n, k = b * CHUNKS + c, c % 2
                    dve.wait_ge(f_silu_done, n + 1)
                    if c >= 2:
                        dve.wait_ge(f_high, n - 1)
                    dve.tensor_tensor(out=f_prod[k], in0=up_ps[k], in1=f_silu[k], op=ALU.mult).then_inc(f_prod_done, 1)
                    dve.wait_ge(f_high, n + 1)
                    dve.tensor_tensor(out=pT_lo[:, k, :], in0=f_prod[k], in1=pT_hi[:, k, :].bitcast(F32),
                                      op=ALU.subtract).then_inc(f_low, 1)
                    if c == 5:
                        row_stats(b + 1)
                    if c == 7:
                        normalise_x(b + 1)
                    if c in (FC, CHUNKS - 1):
                        for t in range(HT):
                            m = (0 if c == FC else HT) + t
                            dve.wait_ge(gate_done, b * TILES + m + 1)
                            dve.tensor_tensor(out=y[:, m, :], in0=y[:, m, :], in1=f_gate[m % 2], op=ALU.mult).then_inc(gated, 1)
                            dve.wait_ge(gated, b * TILES + m + 1)
                            dve.wait_ge(x_again_in[m % 2], (b * HT + m // 2 + 1) * 16)
                            dve.tensor_tensor(out=y[:, m, :], in0=y[:, m, :], in1=x_again[m % 2][:, :], op=ALU.add).then_inc(out_ready, 1)

        @block.gpsimd
        def _(pool):
            def chained(ins, done, count):
                ins.then_inc(pool_chain, 1)
                pool.wait_ge(pool_chain, done + count)
                pool.sem_inc(pool_passed, 1)

            def rsqrt(src, n, mul, add, done):
                xx, aa, yy = rs_x[:, 0:n], rs_a[:, 0:n], rs_y[:, 0:n]
                chained(pool.tensor_scalar(xx, src, mul, add, ALU.mult, ALU.add), done, 1)
                chained(pool.tensor_scalar(yy.bitcast(I32), xx.bitcast(I32), -0.5, RSQRT_SEED, ALU.mult, ALU.add), done, 2)
                for k in range(NEWTON):
                    chained(pool.tensor_tensor(out=aa, in0=yy, in1=yy, op=ALU.mult), done, 4 * k + 3)
                    chained(pool.tensor_tensor(out=aa, in0=aa, in1=xx, op=ALU.mult), done, 4 * k + 4)
                    chained(pool.tensor_scalar(aa, aa, -0.5, 1.5, ALU.mult, ALU.add), done, 4 * k + 5)
                    chained(pool.tensor_tensor(out=yy, in0=aa, in1=yy, op=ALU.mult), done, 4 * k + 6)

            def split(hi, lo, src, high, high_count, done):
                pool.sem_inc(pool_passed, 1)
                pool.tensor_copy(hi, src).then_inc(high, 1)
                pool.wait_ge(high, high_count)
                pool.tensor_tensor(out=lo, in0=src, in1=hi.bitcast(F32), op=ALU.subtract).then_inc(done, 1)

            def low_w(U):
                for c in range(DC):
                    pool.wait_ge(w_high, U * DC + c + 1)
                    pool.tensor_tensor(out=qkv_lo[:, c, :], in0=qkv_raw[:, c, :], in1=qkv_hi[:, c, :].bitcast(F32),
                                       op=ALU.subtract).then_inc(w_split, 1)

            def low_o(U):
                pool.wait_ge(o_high, U + 1)
                pool.tensor_tensor(out=o_lo[:, :], in0=o_raw[:, :], in1=o_hi[:, :].bitcast(F32), op=ALU.subtract).then_inc(o_split, 1)

            def x_norms(row):
                pool.wait_ge(mv_done, (row + 1) * TILES)
                pool.sem_inc(pool_passed, 1)
                rsqrt(mv[:, :, 1], TILES, 1.0, LN_EPS, row * CHAINS * CHAIN)

            x_norms(0)
            low_w(0)
            with pool.Fori(0, B) as b:
                def norms(U, i):
                    t = tile(U, i)
                    if i % TILES == 0:
                        pool.wait_ge(inv_in, (U + 1 + i // TILES) * 16)
                    pool.wait_ge(summed, t)
                    pool.sem_inc(pool_passed, 1)
                    rsqrt(sq_sum[:, :], G + 1, 1.0 / P, RMS_EPS, (b + t) * CHAIN)
                    pool.tensor_tensor(out=rq[:, :], in0=rs_y[:, 0:G + 1], in1=inv_slope[:, :], op=ALU.mult).then_inc(rq_done, 1)

                def split_v(U, i, first):
                    if i == 0 and not first:
                        pool.wait_ge(weighed, U * TURNS)
                    pool.wait_ge(v_staged, tile(U, i))
                    split(v_hi[:, i * P:(i + 1) * P], v_lo[:, i * P:(i + 1) * P], v_nat[:, i % VBUFS, :], v_high, tile(U, i), v_split)

                def low_att(U, i):
                    pool.wait_ge(att_high, U * TILES + i - 1)
                    pool.tensor_tensor(out=attT_lo[:, :], in0=attT[:, :],
                                       in1=attT_hi[:, :].bitcast(F32), op=ALU.subtract).then_inc(att_split, 1)

                def step(U, i, first, last):
                    if not (first and i < 2):
                        low_att(U, i)
                    if not (last and i >= TILES - 2):
                        norms(U, i + 2)
                    if i == 1 and not first:
                        low_o(U)
                    if i == TILES - 3:
                        low_w(U + 1)
                    if i < TILES:
                        split_v(U, i, first)

                def unit(U, first, last):
                    if first:
                        norms(U, 0)
                        norms(U, 1)
                        low_o(U)
                    for i in range(TILES + 2 if last else TILES):
                        step(U, i, first, last)

                units(pool, b, unit)

                def low_gate_up(c):
                    n, k = b * CHUNKS + c, c % 2
                    pool.wait_ge(f_gu_high, n + 1)
                    pool.tensor_tensor(out=f_lo[k][:, 0:NGU], in0=f_raw[k][:, 0:NGU], in1=f_hi[k][:, 0:NGU].bitcast(F32),
                                       op=ALU.subtract).then_inc(f_gu_split, 1)

                def low_down(c):
                    n, k = b * CHUNKS + c, c % 2
                    pool.wait_ge(f_d_high, n + 1)
                    pool.tensor_tensor(out=f_lo[k][:, NGU:NCH], in0=f_raw[k][:, NGU:NCH], in1=f_hi[k][:, NGU:NCH].bitcast(F32),
                                       op=ALU.subtract).then_inc(f_d_split, 1)

                for c in range(CHUNKS):
                    low_gate_up(c)
                    if c:
                        low_down(c - 1)
                    if c == 7:
                        x_norms(b + 1)
                low_down(CHUNKS - 1)


_INS = ["x", "w_qkv", "w_o", "w_ffn", "q_norm", "k_norm", "rel", "slopes", "inv_slopes", "ident"]


def kernel(L0_attn_x, L0_attn_Wq, L0_attn_Wk, L0_attn_Wv, L0_attn_Wo, L0_attn_q_norm_w, L0_attn_k_norm_w,
           L0_ffn_w_gate, L0_ffn_w_up, L0_ffn_w_down):
    import concourse.bacc as bacc
    from concourse.bass_utils import run_bass_kernel_spmd

    def by_chunk(w, parts, n):
        return np.asarray(w).reshape(parts, n, DC, P).transpose(0, 3, 2, 1).reshape(parts, P, DC * n)

    def padded(w):
        full = np.zeros((FC * P, D), np.float32)
        full[:INNER] = np.asarray(w)
        return full

    wq = by_chunk(L0_attn_Wq, HKV, G * P)
    wkv = by_chunk(np.concatenate([np.asarray(L0_attn_Wk).reshape(HKV, P, D), np.asarray(L0_attn_Wv).reshape(HKV, P, D)], 1), HKV, KV)
    ffn = np.concatenate([by_chunk(padded(L0_ffn_w_gate), FC, P), by_chunk(padded(L0_ffn_w_up), FC, P),
                          padded(np.asarray(L0_ffn_w_down).T).reshape(FC, P, D)], 2)
    p, u = np.arange(P)[:, None], np.arange(S)[None, :] - (S - P)
    start = 2.0 ** (-2.0 ** -(np.log2(H) - 3))
    slope = np.array([start * start ** i for i in range(H)], np.float32).reshape(HKV, 1, G)
    arrays = {
        "x": np.asarray(L0_attn_x),
        "w_qkv": np.concatenate([wq.reshape(HKV, P, DC, D), wkv.reshape(HKV, P, DC, KV)], 3).reshape(HKV, P, DC * NW),
        "w_o": np.asarray(L0_attn_Wo).T.reshape(HKV, G, P, D).transpose(0, 2, 1, 3).reshape(HKV, P, G * D),
        "w_ffn": ffn,
        "q_norm": np.asarray(L0_attn_q_norm_w).reshape(P, 1),
        "k_norm": np.asarray(L0_attn_k_norm_w).reshape(P, 1),
        "rel": np.where(u <= p, u - p, -MASK).astype(np.float32),
        "slopes": np.broadcast_to(-slope, (HKV, P, G)),
        "inv_slopes": np.broadcast_to(np.concatenate([1 / slope, np.ones((HKV, 1, 1), np.float32)], 2), (HKV, P, G + 1)),
        "ident": np.eye(P, dtype=np.float32),
    }
    nc = bacc.Bacc("TRN2", target_bir_lowering=False, num_devices=1)
    args, feed = [], {}
    for name in _INS:
        a = np.ascontiguousarray(arrays[name])
        feed[f"{name}_dram"] = a
        args.append(nc.dram_tensor(f"{name}_dram", a.shape, mybir.dt.from_np(a.dtype), kind="ExternalInput").ap())
    out = nc.dram_tensor("out_dram", (B, S, D), F32, kind="ExternalOutput").ap()
    build(nc, *args, out)
    got = run_bass_kernel_spmd(nc, [feed], core_ids=[0])
    return got.results[0]["out_dram"]
```

```python
from contextlib import ExitStack

import numpy as np

import concourse.bass as bass
from concourse import mybir

F32 = mybir.dt.float32
F32R = mybir.dt.float32r
I32 = mybir.dt.int32
ALU = mybir.AluOpType
ACT = mybir.ActivationFunctionType
AX = mybir.AxisListType

P = 128
B, S, D = 2, 1024, 512
TILES = S // P
DC = D // P
H, HKV = 32, 8
G = H // HKV
UNITS = HKV
INNER = 1376
FC = -(-INNER // P)
HALVES = 2
CHUNKS = HALVES * FC
CHAINS = UNITS * TILES + HALVES
HT = TILES // HALVES
BANK = 512
KV = 2 * P
NW = D + KV
NGU = 2 * DC * P
NCH = NGU + D
NQK = (G + 1) * P
VBUFS = 4
GATES = 3
MASK = 2.0 ** 110
LN_EPS, RMS_EPS = 1e-5, 1e-6
RSQRT_SEED, RSQRT_C0, RSQRT_C1 = float(0x5F1FFFF9), 0.703952253 * 2.38924456, 0.703952253
CHAIN = 12

HEAD_CHUNKS = [-(-(i + 1) * P // BANK) for i in range(TILES)]
SCORE_AT = [G * sum(HEAD_CHUNKS[:i]) for i in range(TILES + 1)]
SCORES = SCORE_AT[TILES]
TURNS = TILES * (TILES + 1) // 2
BEFORE = [TILES] + list(range(1, TILES))
RING_PER_STEP = 2
TURN_AT = [sum(BEFORE[1:i + 1]) - BEFORE[i] for i in range(TILES)] + [TURNS - TILES]
RBANKS = 3
RING = TURNS + RING_PER_STEP * TILES
RING_AT = [RING_PER_STEP - TILES]
for _i in range(TILES):
    RING_AT.append(RING_AT[-1] + BEFORE[_i] + RING_PER_STEP)
RING_AT[TILES] -= RING_PER_STEP
SKIPS = [RING_AT[2], RING_AT[5]]
RING_BANK = [(r + sum(r >= skip for skip in SKIPS)) % RBANKS for r in range(RING)]
assert (RING + len(SKIPS)) % RBANKS == 0
SLOTS = 4
LAG = 2


def ring_bank(r):
    return RING_BANK[r % RING]


def last_use(r):
    return next(q for q in range(r - 1, r - 2 * RBANKS, -1) if ring_bank(q) == ring_bank(r))


def shape_of_step(i, first):
    chunks = G * HEAD_CHUNKS[i] if i < TILES else 0
    turns = 0 if first and i == 0 else TILES if i == TILES else BEFORE[i]
    return chunks, turns, max(chunks, turns + LAG if turns else 0)


def build(nc, x, w_qkv, w_o, w_ffn, q_norm, k_norm, rel, slopes, inv_slopes, ident_in, out):
    ctx = ExitStack()
    with ctx:
        def sb(name, shape, dt=F32):
            return ctx.enter_context(nc.sbuf_tensor(name, shape, dt))

        def psum(name, shape):
            return ctx.enter_context(nc.psum_tensor(name, shape, F32))

        def sem(name):
            return ctx.enter_context(nc.semaphore(name))

        xT_hi, xT_lo = sb("xT_hi", [P, DC, S], F32R), sb("xT_lo", [P, DC, S], F32R)
        y = sb("y", [P, TILES, D])
        qkv_raw, o_raw = sb("qkv_raw", [P, DC, NW]), sb("o_raw", [P, G * D])
        qkv_hi, qkv_lo = sb("qkv_hi", [P, DC, NW], F32R), sb("qkv_lo", [P, DC, NW], F32R)
        o_hi, o_lo = sb("o_hi", [P, G * D], F32R), sb("o_lo", [P, G * D], F32R)
        kv_hi, kv_lo = sb("kv_hi", [P, 2 * S], F32R), sb("kv_lo", [P, 2 * S], F32R)
        kT_hi, kT_lo = kv_hi[:, 0:S], kv_lo[:, 0:S]
        v_hi, v_lo = kv_hi[:, S:2 * S], kv_lo[:, S:2 * S]
        qT_hi, qT_lo = sb("qT_hi", [P, 2, G * P], F32R), sb("qT_lo", [P, 2, G * P], F32R)
        probs = [sb("probs0", [P, G, S - P]), sb("probs1", [P, G, S])]
        pT_hi, pT_lo = sb("pT_hi", [P, SLOTS, G * P], F32R), sb("pT_lo", [P, SLOTS, G * P], F32R)
        attT_hi, attT_lo = sb("attT_hi", [P, G * P], F32R), sb("attT_lo", [P, G * P], F32R)
        natural = sb("natural", [P, 3 * NQK])
        qk = [natural[:, k * NQK:(k + 1) * NQK] for k in range(2)]
        qk_sq = natural[:, 2 * NQK:3 * NQK]
        v_nat = sb("v_nat", [P, VBUFS, P])
        rel_sb, ident = sb("rel_sb", [P, S]), sb("ident", [P, P])
        slope, inv_slope = sb("slope", [P, G]), sb("inv_slope", [P, G + 1])
        norm_w, wcol = sb("norm_w", [P, 2]), sb("wcol", [P, 1])
        low_min = sb("low_min", [P, 2, G, 2])
        row_sum, rec = sb("row_sum", [P, 2, G]), sb("rec", [P, G])
        sq_sum, rq = sb("sq_sum", [P, G + 1]), sb("rq", [P, G + 1])
        rs_x, rs_a, rs_y = [sb(name, [P, TILES + G + 1]) for name in ("rs_x", "rs_a", "rs_y")]
        stats, mv = sb("stats", [P, TILES, 6]), sb("mv", [P, TILES, 2])

        w_raw = qkv_raw[:, :, :].rearrange("p c n -> p (c n)")
        f_raw = [w_raw[:, k * NCH:(k + 1) * NCH] for k in range(2)]
        gu_hi, gu_lo = [[w[:, k * NGU:(k + 1) * NGU] for k in range(2)] for w in (kv_hi, kv_lo)]
        d_hi, d_lo = [[w[:, k, :] for k in range(2)] for w in (qT_hi, qT_lo)]
        probs0 = probs[0][:, :, :].rearrange("p g n -> p (g n)")
        f_silu = [probs0[:, k * BANK:(k + 1) * BANK] for k in range(2)]
        f_prod = [probs0[:, (2 + k) * BANK:(3 + k) * BANK] for k in range(2)]
        f_gate = [probs0[:, (4 + k) * BANK:(5 + k) * BANK] for k in range(GATES)]
        x_again = o_raw[:, :].rearrange("p (t d) -> p t d", d=D)
        xn = probs[1][:, :, :].rearrange("p g n -> p (g n)").rearrange("p (t d) -> p t d", d=D)

        qkv_ps = psum("qkv_ps", [P, 2 * BANK])
        score_ps = psum("score_ps", [P, 2, BANK])
        ring_ps = psum("ring_ps", [P, RBANKS, BANK])
        out_ps = psum("out_ps", [P, BANK])
        gate_ps = [score_ps[:, k, :] for k in range(2)]
        up_ps = [qkv_ps[:, k * BANK:(k + 1) * BANK] for k in range(2)]
        down_ps = [ring_ps[:, k, :] for k in range(RBANKS)] + [out_ps[:, :]]
        xT_ps = gate_ps + up_ps + down_ps
        first_ps = score_ps[:, :, :].rearrange("p a n -> p (a n)")
        assert HT == len(down_ps)

        ident_loaded, rel_in, w_in = sem("ident_loaded"), sem("rel_in"), sem("w_in")
        x_in = [sem("x_in0"), sem("x_in1")]
        x_again_in = sem("x_again_in")
        qkv_in, o_in, slope_in, inv_in = sem("qkv_in"), sem("o_in"), sem("slope_in"), sem("inv_in")
        f_in = [sem("f_in0"), sem("f_in1")]
        stats_done, mv_done = sem("stats_done"), sem("mv_done")
        xn_done, xT_turned, xT_high, xT_low = sem("xn_done"), sem("xT_turned"), sem("xT_high"), sem("xT_low")
        y_free, y_zero = sem("y_free"), sem("y_zero")
        w_high, w_split, o_high = sem("w_high"), sem("w_split"), sem("o_high")
        o_split = sem("o_split")
        projected, squared, summed, rq_done = sem("projected"), sem("squared"), sem("summed"), sem("rq_done")
        qk_done, v_staged, v_high, v_split = sem("qk_done"), sem("v_staged"), sem("v_high"), sem("v_split")
        scored, biased, exped = sem("scored"), sem("biased"), sem("exped")
        ring_full, ring_high, ring_lowd = sem("ring_full"), sem("ring_high"), sem("ring_lowd")
        weighed, rec_done, divided = sem("weighed"), sem("rec_done"), sem("divided")
        att_high, att_split = sem("att_high"), sem("att_split")
        out_proj, y_added = sem("out_proj"), sem("y_added")
        pool_chain = sem("pool_chain")
        f_gu_high, f_d_high = sem("f_gu_high"), sem("f_d_high")
        f_gu_split, f_d_split = sem("f_gu_split"), sem("f_d_split")
        f_gu_done, f_silu_done, f_prod_done = sem("f_gu_done"), sem("f_silu_done"), sem("f_prod_done")
        f_high, f_low, f_down = sem("f_high"), sem("f_low"), sem("f_down")
        gate_done, gated, out_ready, stored = sem("gate_done"), sem("gated"), sem("out_ready"), sem("stored")
        wcol_done = sem("wcol_done")
        sp_passed, dve_passed, pool_passed = sem("sp_passed"), sem("dve_passed"), sem("pool_passed")

        block = ctx.enter_context(nc.Block())

        def units(eng, b, body):
            body(b * UNITS, True, False)
            with eng.Fori(1, UNITS - 1) as g:
                body(b * UNITS + g, False, False)
            body(b * UNITS + UNITS - 1, False, True)

        def feed(eng, body):
            mid = FC // 2
            body(0, 0, 0)
            body(0, 1, 0)
            with eng.Fori(1, mid) as q:
                body(q, 0, 0)
                body(q, 1, 0)
            body(mid, 0, 0)
            body(mid, 1, 1)
            body(mid + 1, 0, 1)
            body(mid + 1, 1, 1)
            with eng.Fori(mid + 2, CHUNKS // 2 - 1) as q:
                body(q, 0, 1)
                body(q, 1, 1)
            body(CHUNKS // 2 - 1, 0, 1)
            body(CHUNKS // 2 - 1, 1, 1)

        def half_of(c):
            return 0 if c == FC else 1

        o_parts = [slice(k * 2 * D, (k + 1) * 2 * D) for k in range(2)]

        def known(q, k):
            return 2 * q + k if isinstance(q, int) else -1

        def tile(U, i):
            return U * TILES + i + 1

        @block.sync
        def _(sp):
            def alone(sem, value):
                sp.wait_ge(sem, value)
                sp.sem_inc(sp_passed, 1)

            def load_unit(g):
                sp.dma_start(qkv_raw[:, :, :].rearrange("p c n -> p (c n)"),
                             w_qkv[bass.ds(g, 1), :, :].rearrange("a p n -> p (a n)")).then_inc(qkv_in, 16)

            def load_o(g):
                sp.dma_start(o_raw[:, :], w_o[bass.ds(g, 1), :, :].rearrange("a p n -> p (a n)")).then_inc(o_in, 16)

            def load_inv(g):
                sp.dma_start(inv_slope[:, :], inv_slopes[bass.ds(g, 1), :, :].rearrange("a p n -> p (a n)")).then_inc(inv_in, 16)

            def load_slope(g):
                sp.dma_start(slope[:, :], slopes[bass.ds(g, 1), :, :].rearrange("a p n -> p (a n)")).then_inc(slope_in, 16)

            def load_x(to, row, half, sem):
                sp.dma_start(to, x[bass.ds(row, 1), half * BANK:(half + 1) * BANK, :].rearrange("a (t p) d -> p (a t) d", p=P)
                             ).then_inc(sem, 16)

            load_x(xn[:, 0:HT, :], 0, 0, x_in[0])
            sp.dma_start(ident[:, :], ident_in).then_inc(ident_loaded, 16)
            sp.dma_start(norm_w[:, 0:1], q_norm).then_inc(w_in, 16)
            sp.dma_start(norm_w[:, 1:2], k_norm).then_inc(w_in, 16)
            load_x(xn[:, HT:TILES, :], 0, 1, x_in[1])
            load_unit(0)
            load_inv(0)
            sp.dma_start(rel_sb[:, :], rel).then_inc(rel_in, 16)
            load_slope(0)
            load_o(0)
            sp.sem_inc(y_free, 1)

            with sp.Fori(0, B) as b:
                with sp.Fori(0, UNITS - 1) as g:
                    U = b * UNITS + g
                    alone(w_split, (U + 1) * DC)
                    load_unit(g + 1)
                    alone(o_split, 2 * (U + 1))
                    load_o(g + 1)
                    alone(rq_done, (U + 1) * TILES)
                    load_inv(g + 1)
                    alone(biased, (U + 1) * SCORES)
                    load_slope(g + 1)

                U = b * UNITS + UNITS - 1
                alone(w_split, (U + 1) * DC)
                load_unit(0)
                alone(o_split, 2 * (U + 1))
                load_x(x_again, b, 0, x_again_in)
                alone(rq_done, (U + 1) * TILES)
                load_inv(0)
                alone(w_split, (U + 2) * DC)

                def load_chunk(q, k, half):
                    c = 2 * q + k
                    if known(q, k) not in (0, 1):
                        alone(f_d_split, b * CHUNKS + c - 1)
                    sp.dma_start(f_raw[k], w_ffn[bass.ds(c - half * FC, 1), :, :].rearrange("a p n -> p (a n)")
                                 ).then_inc(f_in[k], 16)
                    if known(q, k) == 1:
                        alone(biased, (b + 1) * UNITS * SCORES)
                        load_slope(0)
                    if known(q, k) == FC - 1:
                        for h in range(HALVES):
                            load_x(xn[:, h * HT:(h + 1) * HT, :], B - 1, h, x_in[h])
                    if known(q, k) == CHUNKS - 2:
                        store(0)
                        load_x(x_again, b, 1, x_again_in)

                def store(half):
                    for m in range(half * HT, (half + 1) * HT):
                        alone(out_ready, b * TILES + m + 1)
                        sp.dma_start(out[bass.ds(b, 1), m * P:(m + 1) * P, :].rearrange("a p d -> p (a d)"),
                                     y[:, m, :]).then_inc(stored, 16)

                feed(sp, load_chunk)
                alone(f_d_split, (b + 1) * CHUNKS)
                store(1)
                load_o(0)
                alone(stored, (b + 1) * TILES * 16)
                sp.sem_inc(y_free, 1)
            sp.wait_ge(o_in, (B * UNITS + 1) * 16)

        @block.tensor
        def _(pe):
            def ring_free(U, r, first):
                q = last_use(r)
                if not (first and q < 0):
                    pe.wait_ge(ring_lowd, U * RING + q + 1)

            def project(U, i, acc, early):
                if not early:
                    pe.wait_ge(qk_done, tile(U, i) - 1)
                    pe.wait_ge(v_staged, tile(U, i) - 1)
                for c in range(DC):
                    if i == 0:
                        pe.wait_ge(w_split, U * DC + c + 1)
                    for xT, w in ((xT_hi, qkv_hi), (xT_hi, qkv_lo), (xT_lo, qkv_hi)):
                        a = xT[:, c, i * P:(i + 1) * P]
                        go, end = c == 0 and xT is xT_hi and w is qkv_hi, c == DC - 1 and xT is xT_lo
                        pe.matmul(acc[:, 0:BANK], a, w[:, c, 0:D], start=go, stop=end)
                        mm = pe.matmul(acc[:, BANK:BANK + KV], a, w[:, c, D:NW], start=go, stop=end)
                mm.then_inc(projected, 1)

            def turn_q(U, i, r, first, t):
                ring_free(U, r, first)
                pe.wait_ge(qk_done, t)
                for h in range(G):
                    tr = pe.transpose(ring_ps[:, ring_bank(r), h * P:(h + 1) * P], qk[i % 2][:, h * P:(h + 1) * P], ident[:, :])
                tr.then_inc(ring_full, 1)

            def turn_k(U, i, r, first):
                ring_free(U, r, first)
                pe.transpose(ring_ps[:, ring_bank(r), 0:P], qk[i % 2][:, G * P:NQK], ident[:, :]).then_inc(ring_full, 1)

            def scores(U, i, k, first):
                n = SCORE_AT[i] + k
                h, part = k // HEAD_CHUNKS[i], k % HEAD_CHUNKS[i]
                lo, hi = part * BANK, min((part + 1) * BANK, (i + 1) * P)
                if k == 0:
                    low = 1 if first and i == 0 else RING_AT[i] - 1
                    pe.wait_ge(ring_lowd, U * RING + low + 1)
                if not (first and n < 2):
                    pe.wait_ge(biased, U * SCORES + n - 1)
                for q, kt in ((qT_hi, kT_hi), (qT_hi, kT_lo), (qT_lo, kT_hi)):
                    mm = pe.matmul(score_ps[:, n % 2, 0:hi - lo], q[:, i % 2, h * P:(h + 1) * P], kt[:, lo:hi],
                                   start=(q is qT_hi and kt is kT_hi), stop=(q is qT_lo))
                mm.then_inc(scored, 1)

            def turn_probs(U, i, j, first):
                r, p = RING_AT[i] + j, (i - 1) % TILES
                ring_free(U, r, first)
                for h in range(G):
                    if j == 0:
                        pe.wait_ge(divided, (U * TILES + i - 1) * G + h + 1)
                    tr = pe.transpose(ring_ps[:, ring_bank(r), h * P:(h + 1) * P],
                                      probs[p % 2][:, h, j * P:(j + 1) * P], ident[:, :])
                tr.then_inc(ring_full, 1)

            def weigh(U, i, j, turns, first):
                if j == 0:
                    pe.wait_ge(v_split, U * TILES + i)
                    if not (first and i < 2):
                        pe.wait_ge(y_added, U * TILES + i - 1)
                pe.wait_ge(ring_lowd, U * RING + RING_AT[i] + j + 1)
                slot = (TURN_AT[i] + j) % SLOTS
                for v, pt in ((v_hi, pT_hi), (v_hi, pT_lo), (v_lo, pT_hi)):
                    mm = pe.matmul(out_ps[:, :], v[:, j * P:(j + 1) * P], pt[:, slot, :],
                                   start=(j == 0 and v is v_hi and pt is pT_hi),
                                   stop=(j == turns - 1 and v is v_lo))
                mm.then_inc(weighed, 1)

            def out_project(U, i):
                pe.wait_ge(att_split, U * TILES + i - 1)
                for h in range(G):
                    if i == 2 and h % 2 == 0:
                        pe.wait_ge(o_split, 2 * U + h // 2 + 1)
                    for a, w in ((attT_hi, o_hi), (attT_hi, o_lo), (attT_lo, o_hi)):
                        mm = pe.matmul(out_ps[:, :], a[:, h * P:(h + 1) * P], w[:, h * D:(h + 1) * D],
                                       start=(h == 0 and a is attT_hi and w is o_hi),
                                       stop=(h == G - 1 and a is attT_lo))
                mm.then_inc(out_proj, 1)

            def step(U, i, first, last):
                ahead = not (last and i >= TILES - 1)
                if first and i == 0:
                    for k in range(G):
                        scores(U, 0, k, True)
                    pe.wait_ge(biased, U * SCORES + G)
                    project(U, 2, first_ps, True)
                    turn_q(U, 1, RING_AT[0] + BEFORE[0], True, tile(U, 1))
                    turn_k(U, 1, RING_AT[0] + BEFORE[0] + 1, True)
                    project(U, 3, qkv_ps, True)
                    return
                if first and i == 1:
                    pe.wait_ge(qk_done, tile(U, 2))
                    pe.wait_ge(v_staged, tile(U, 2))
                elif not (last and i >= TILES - 2):
                    project(U + (i + 2) // TILES, (i + 2) % TILES, qkv_ps, False)
                late = last and TILES - 2 <= i <= TILES
                if not (first and i < 2) and not late:
                    out_project(U, i)
                if i > TILES:
                    return
                chunks, turns, slots = shape_of_step(i, first)
                for k in range(slots):
                    if k < chunks and not (late and k == 1):
                        scores(U, i, k, first)
                    if late and k == 0:
                        if chunks:
                            scores(U, i, 1, first)
                        out_project(U, i)
                    if k < turns:
                        turn_probs(U, i, k, first)
                    if ahead and turns and k == turns + 1:
                        turn_q(U, (i + 1) % TILES, RING_AT[i] + BEFORE[i], first, tile(U, i + 1))
                        turn_k(U, (i + 1) % TILES, RING_AT[i] + BEFORE[i] + 1, first)
                    if 0 <= k - LAG < turns:
                        weigh(U, i, k - LAG, turns, first)

            pe.wait_ge(ident_loaded, 16)

            def turn_x(row, t):
                pe.wait_ge(xn_done, row * TILES + t + 1)
                for c in range(DC):
                    tr = pe.transpose(xT_ps[t][:, c * P:(c + 1) * P], xn[:, t, c * P:(c + 1) * P], ident[:, :])
                tr.then_inc(xT_turned, 1)

            for t in range(HT):
                turn_x(0, t)
            with pe.Fori(0, B) as b:
                def gate_up(q, k, half=0):
                    n = b * CHUNKS + 2 * q + k
                    pe.wait_ge(f_gu_split, n + 1)
                    if known(q, k) not in (0, 1):
                        pe.wait_ge(f_prod_done, n - 1)
                    for part, acc in ((0, gate_ps[k]), (1, up_ps[k])):
                        for d in range(DC):
                            for w, xT in ((gu_hi, xT_hi), (gu_hi, xT_lo), (gu_lo, xT_hi)):
                                at = (part * DC + d) * P
                                mm = pe.matmul(acc, w[k][:, at:at + P], xT[:, d, half * BANK:(half + 1) * BANK],
                                               start=(d == 0 and w is gu_hi and xT is xT_hi),
                                               stop=(d == DC - 1 and w is gu_lo))
                    mm.then_inc(f_gu_done, 1)

                def down(q, k):
                    n, c = b * CHUNKS + 2 * q + k, known(q, k)
                    pe.wait_ge(f_d_split, n + 1)
                    pe.wait_ge(f_low, n + 1)
                    if c == 0:
                        pe.wait_ge(y_added, (b + 1) * UNITS * TILES)
                    if c == FC:
                        pe.wait_ge(gate_done, b * TILES + HT)
                    for t in range(HT):
                        for a, w in ((pT_hi, d_hi), (pT_hi, d_lo), (pT_lo, d_hi)):
                            mm = pe.matmul(down_ps[t], a[:, k, t * P:(t + 1) * P], w[k],
                                           start=(c in (0, FC) and a is pT_hi and w is d_hi),
                                           stop=(c in (FC - 1, CHUNKS - 1) and a is pT_lo))
                        mm.then_inc(f_down, 1)

                def chunk(q, k, half):
                    if known(q, k) == 0:
                        return
                    gate_up(q, k, half)
                    down(q if k else q - 1, 1 - k)
                    if known(q, k) == CHUNKS - 1:
                        pe.wait_ge(f_prod_done, (b + 1) * CHUNKS)
                        for t in range(HT):
                            turn_x(b + 1, t)
                        down(q, k)

                def unit(U, first, last):
                    if first:
                        pe.wait_ge(xT_low, b * TILES + 2)
                        project(U, 0, first_ps, True)
                        for i in range(HT, TILES):
                            turn_x(b, i)
                        pe.wait_ge(xT_low, b * TILES + HT)
                        project(U, 1, qkv_ps, True)
                        pe.wait_ge(xT_low, b * TILES + TILES)
                        turn_q(U, 0, 0, True, tile(U, 0))
                        turn_k(U, 0, 1, True)
                    for i in range(TILES + 2 if last else TILES):
                        if i == TILES + 1:
                            gate_up(0, 0)
                        step(U, i, first, last)

                units(pe, b, unit)
                feed(pe, chunk)

        @block.scalar
        def _(act):
            def square(acc, t, first):
                act.wait_ge(projected, t)
                if not first:
                    act.wait_ge(summed, t - 1)
                act.activation(qk_sq, acc[:, 0:(G + 1) * P], ACT.Square).then_inc(squared, 1)

            def stage_v(acc, i, t, early):
                if not early:
                    act.wait_ge(v_split, t - VBUFS)
                act.activation(v_nat[:, i % VBUFS, :], acc[:, BANK + P:BANK + KV], ACT.Copy).then_inc(v_staged, 1)

            def high_q(U, i, r):
                act.wait_ge(ring_full, U * RING + r + 1)
                act.activation(qT_hi[:, i % 2, :], ring_ps[:, ring_bank(r), :],
                               ACT.Copy, scale=wcol[:, 0:1]).then_inc(ring_high, 1)

            def high_k(U, i, r):
                act.wait_ge(ring_full, U * RING + r + 1)
                act.activation(kT_hi[:, i * P:(i + 1) * P], ring_ps[:, ring_bank(r), 0:P], ACT.Copy).then_inc(ring_high, 1)

            def exp(U, i, h):
                act.wait_ge(biased, U * SCORES + SCORE_AT[i] + (h + 1) * HEAD_CHUNKS[i])
                row = probs[i % 2][:, h, 0:(i + 1) * P]
                act.activation(row, row, ACT.Exp, scale=-1.0, bias=low_min[:, i % 2, h, HEAD_CHUNKS[i] - 1:HEAD_CHUNKS[i]],
                               accum_out=row_sum[:, i % 2, h:h + 1]).then_inc(exped, 1)

            def high_probs(U, i, j, first):
                r, n = RING_AT[i] + j, TURN_AT[i] + j
                act.wait_ge(ring_full, U * RING + r + 1)
                if not (first and n < SLOTS):
                    act.wait_ge(weighed, U * TURNS + n - SLOTS + 1)
                act.activation(pT_hi[:, n % SLOTS, :], ring_ps[:, ring_bank(r), :], ACT.Copy).then_inc(ring_high, 1)

            def high_att(U, i):
                act.wait_ge(weighed, U * TURNS + (TURN_AT[i] if i <= TILES else TURNS))
                act.activation(attT_hi[:, :], out_ps[:, :], ACT.Copy).then_inc(att_high, 1)

            def high_o(U, part, used):
                if part == 0:
                    act.wait_ge(o_in, (U + 1) * 16)
                    if used:
                        act.wait_ge(out_proj, U * TILES)
                act.activation(o_hi[:, o_parts[part]], o_raw[:, o_parts[part]], ACT.Copy).then_inc(o_high, 1)

            def high_w(U, c):
                act.activation(qkv_hi[:, c, :], qkv_raw[:, c, :], ACT.Copy).then_inc(w_high, 1)

            act.wait_ge(qkv_in, 16)
            for c in range(DC):
                high_w(0, c)
            act.wait_ge(wcol_done, 1)

            def high_x(row, t):
                act.wait_ge(xT_turned, row * TILES + t + 1)
                act.activation(xT_hi[:, :, t * P:(t + 1) * P],
                               xT_ps[t].rearrange("p (c n) -> p c n", c=DC), ACT.Copy).then_inc(xT_high, 1)

            for t in range(HT):
                high_x(0, t)
            with act.Fori(0, B) as b:
                def high_gate_up(q, k):
                    n = b * CHUNKS + 2 * q + k
                    act.wait_ge(f_in[k], (b * (CHUNKS // 2) + q + 1) * 16)
                    if known(q, k) == 0:
                        act.wait_ge(biased, (b + 1) * UNITS * SCORES)
                    elif known(q, k) == 1:
                        act.wait_ge(weighed, (b + 1) * UNITS * TURNS)
                    else:
                        act.wait_ge(f_gu_done, n - 1)
                    act.activation(gu_hi[k], f_raw[k][:, 0:NGU], ACT.Copy).then_inc(f_gu_high, 1)

                def high_down(q, k):
                    n = b * CHUNKS + 2 * q + k
                    if known(q, k) not in (0, 1):
                        act.wait_ge(f_down, (n - 1) * HT)
                    act.activation(d_hi[k], f_raw[k][:, NGU:NCH], ACT.Copy).then_inc(f_d_high, 1)

                def step(U, i, first, last):
                    ahead = not (last and i >= TILES - 1)
                    if first and i == 0:
                        for h in range(G):
                            exp(U, 0, h)
                        high_q(U, 1, RING_AT[0] + BEFORE[0])
                        high_k(U, 1, RING_AT[0] + BEFORE[0] + 1)
                        square(first_ps, tile(U, 2), False)
                        stage_v(first_ps, 2, tile(U, 2), True)
                        high_o(U, 0, False)
                        high_o(U, 1, False)
                        square(qkv_ps, tile(U, 3), False)
                        stage_v(qkv_ps, 3, tile(U, 3), True)
                        return
                    if not (first and i < 2):
                        high_att(U, i)
                    if i > TILES:
                        high_gate_up(0, 1)
                        high_down(0, 1)
                        return
                    if not (last and i >= TILES - 2) and not (first and i == 1):
                        square(qkv_ps, tile(U, i + 2), False)
                        stage_v(qkv_ps, (i + 2) % TILES, tile(U, i + 2), False)
                    chunks, turns, slots = shape_of_step(i, first)
                    for k in range(slots + 1):
                        if k < turns:
                            high_probs(U, i, k, first)
                        if ahead and turns and k == turns + 1:
                            high_q(U, (i + 1) % TILES, RING_AT[i] + BEFORE[i])
                            high_k(U, (i + 1) % TILES, RING_AT[i] + BEFORE[i] + 1)
                        if 1 <= k <= chunks and k % HEAD_CHUNKS[i] == 0:
                            exp(U, i, k // HEAD_CHUNKS[i] - 1)
                        if k < 2 and i == 1 and not first:
                            high_o(U, k, True)
                        if i == TILES - 3 and k < DC:
                            if k == 0:
                                act.wait_ge(qkv_in, (U + 2) * 16)
                                act.wait_ge(projected, tile(U, TILES - 1))
                            high_w(U + 1, k)
                        if i == TILES and k == LAG + 1:
                            high_gate_up(0, 0)
                            high_down(0, 0)

                def unit(U, first, last):
                    if first:
                        square(first_ps, tile(U, 0), True)
                        stage_v(first_ps, 0, tile(U, 0), True)
                        for t in range(HT, TILES):
                            high_x(b, t)
                        square(qkv_ps, tile(U, 1), False)
                        stage_v(qkv_ps, 1, tile(U, 1), True)
                        high_q(U, 0, 0)
                        high_k(U, 0, 1)
                    for i in range(TILES + 2 if last else TILES):
                        step(U, i, first, last)

                def chunk(q, k, half):
                    n, c = b * CHUNKS + 2 * q + k, known(q, k)
                    act.wait_ge(f_gu_done, n + 1)
                    act.activation(f_silu[k], gate_ps[k], ACT.Silu).then_inc(f_silu_done, 1)
                    act.wait_ge(f_prod_done, n + 1)
                    if c not in (0, 1):
                        act.wait_ge(f_down, (n - 1) * HT)
                    act.activation(pT_hi[:, k, :], f_prod[k], ACT.Copy).then_inc(f_high, 1)
                    if c not in (0, CHUNKS - 1):
                        high_down(q + k, 1 - k)
                    if c not in (CHUNKS - 2, CHUNKS - 1):
                        high_gate_up(q + 1, k)
                    if c == CHUNKS - 1:
                        for t in range(HT):
                            high_x(b + 1, t)
                    if c in (FC, CHUNKS - 1):
                        for t in range(HT):
                            m = half_of(c) * HT + t
                            act.wait_ge(f_down, (b * CHUNKS + (half_of(c) + 1) * FC - 1) * HT + t + 1)
                            if m >= GATES:
                                act.wait_ge(gated, b * TILES + m - GATES + 1)
                            act.activation(f_gate[m % GATES], down_ps[t], ACT.Silu).then_inc(gate_done, 1)

                units(act, b, unit)
                feed(act, chunk)

        @block.vector
        def _(dve):
            def sum_squares(t, first):
                dve.wait_ge(squared, t)
                if not first:
                    dve.wait_ge(rq_done, t - 1)
                dve.tensor_reduce(sq_sum[:, :], qk_sq.rearrange("p (g n) -> p g n", g=G + 1),
                                  AX.X, ALU.add).then_inc(summed, 1)

            def scale_qk(acc, i, t):
                dve.wait_ge(rq_done, t)
                dve.wait_ge(v_staged, t)
                dve.tensor_tensor(out=qk[i % 2].rearrange("p (g n) -> p g n", g=G + 1),
                                  in0=acc[:, 0:(G + 1) * P].rearrange("p (g n) -> p g n", g=G + 1),
                                  in1=rq[:, :].unsqueeze(2).to_broadcast([P, G + 1, P]), op=ALU.mult).then_inc(qk_done, 1)

            def low_q(U, i, r):
                dve.wait_ge(ring_high, U * RING + r + 1)
                dve.scalar_tensor_tensor(out=qT_lo[:, i % 2, :], in0=ring_ps[:, ring_bank(r), :],
                                         scalar=wcol[:, 0:1], in1=qT_hi[:, i % 2, :].bitcast(F32),
                                         op0=ALU.mult, op1=ALU.subtract).then_inc(ring_lowd, 1)

            def low_k(U, i, r):
                dve.wait_ge(ring_high, U * RING + r + 1)
                dve.tensor_tensor(out=kT_lo[:, i * P:(i + 1) * P], in0=ring_ps[:, ring_bank(r), 0:P],
                                  in1=kT_hi[:, i * P:(i + 1) * P].bitcast(F32), op=ALU.subtract).then_inc(ring_lowd, 1)

            def bias(U, i, k):
                n = SCORE_AT[i] + k
                h, part = k // HEAD_CHUNKS[i], k % HEAD_CHUNKS[i]
                lo, hi = part * BANK, min((part + 1) * BANK, (i + 1) * P)
                if k == 0 and i == 0:
                    dve.wait_ge(slope_in, (U + 1) * 16)
                if part:
                    dve.wait_ge(biased, U * SCORES + n)
                dve.wait_ge(scored, U * SCORES + n + 1)
                dve.sem_inc(dve_passed, 1)
                at = S - (i + 1) * P + lo
                dve.tensor_tensor_reduce(
                    out=probs[i % 2][:, h, lo:hi], in0=score_ps[:, n % 2, 0:hi - lo], in1=rel_sb[:, at:at + hi - lo],
                    scale=slope[:, h:h + 1], scalar=low_min[:, i % 2, h, 0:1] if part else 3.0e38,
                    op0=ALU.add, op1=ALU.min, accum_out=low_min[:, i % 2, h, part:part + 1]).then_inc(biased, 1)

            def low_probs(U, i, j):
                r, n = RING_AT[i] + j, TURN_AT[i] + j
                dve.wait_ge(ring_high, U * RING + r + 1)
                dve.tensor_tensor(out=pT_lo[:, n % SLOTS, :], in0=ring_ps[:, ring_bank(r), :],
                                  in1=pT_hi[:, n % SLOTS, :].bitcast(F32), op=ALU.subtract).then_inc(ring_lowd, 1)

            def divide(U, i):
                dve.wait_ge(exped, (U * TILES + i + 1) * G)
                dve.reciprocal(rec[:, :], row_sum[:, i % 2, :]).then_inc(rec_done, 1)
                dve.wait_ge(rec_done, U * TILES + i + 1)
                for h in range(G):
                    row = probs[i % 2][:, h, 0:(i + 1) * P]
                    dve.tensor_scalar(row, row, rec[:, h:h + 1], None, ALU.mult).then_inc(divided, 1)

            def low_att(U, i):
                dve.wait_ge(att_high, U * TILES + i - 1)
                dve.tensor_tensor(out=attT_lo[:, :], in0=out_ps[:, :], in1=attT_hi[:, :].bitcast(F32),
                                  op=ALU.subtract).then_inc(att_split, 1)

            def add_y(U, i, copy):
                p = (i - 2) % TILES
                dve.wait_ge(out_proj, U * TILES + i - 1)
                if copy:
                    dve.tensor_copy(y[:, p, :], out_ps[:, :]).then_inc(y_added, 1)
                else:
                    dve.tensor_tensor(out=y[:, p, :], in0=out_ps[:, :], in1=y[:, p, :], op=ALU.add).then_inc(y_added, 1)

            def row_stats(row):
                for half in range(HALVES):
                    dve.wait_ge(x_in[half], (row + 1) * 16)
                    for t in range(half * HT, (half + 1) * HT):
                        dve.bn_stats(stats[:, t, :], xn[:, t, :]).then_inc(stats_done, 1)
                    dve.wait_ge(stats_done, row * TILES + (half + 1) * HT)
                    dve.sem_inc(dve_passed, 1)
                    for t in range(half * HT, (half + 1) * HT):
                        dve.bn_aggr(mv[:, t, :], stats[:, t, :]).then_inc(mv_done, 1)

            def normalise_x(row, half):
                dve.wait_ge(pool_chain, (row * CHAINS + half + 1) * CHAIN)
                for t in range(half * HT, (half + 1) * HT):
                    dve.tensor_scalar(xn[:, t, :], xn[:, t, :], mv[:, t, 0:1], rs_y[:, t:t + 1],
                                      ALU.subtract, ALU.mult).then_inc(xn_done, 1)

            row_stats(0)
            dve.wait_ge(w_in, 32)
            dve.scalar_tensor_tensor(out=wcol[:, :], in0=norm_w[:, 0:1], scalar=float(P) ** -0.5, in1=norm_w[:, 1:2],
                                     op0=ALU.mult, op1=ALU.mult).then_inc(wcol_done, 1)
            dve.wait_ge(wcol_done, 1)

            def low_x(row, t):
                dve.wait_ge(xT_high, row * TILES + t + 1)
                dve.tensor_tensor(out=xT_lo[:, :, t * P:(t + 1) * P],
                                  in0=xT_ps[t].rearrange("p (c n) -> p c n", c=DC),
                                  in1=xT_hi[:, :, t * P:(t + 1) * P].bitcast(F32), op=ALU.subtract).then_inc(xT_low, 1)

            normalise_x(0, 0)
            for c in range(DC // 2):
                dve.wait_ge(w_high, c + 1)
                dve.tensor_tensor(out=qkv_lo[:, c, :], in0=qkv_raw[:, c, :], in1=qkv_hi[:, c, :].bitcast(F32),
                                  op=ALU.subtract).then_inc(w_split, 1)
            for t in range(HT):
                low_x(0, t)
            dve.wait_ge(rel_in, 16)
            with dve.Fori(0, B) as b:
                def step(U, i, first, last):
                    ahead = not (last and i >= TILES - 1)
                    if first and i == 0:
                        for k in range(G):
                            bias(U, 0, k)
                        scale_qk(qkv_ps, 1, tile(U, 1))
                        low_q(U, 1, RING_AT[0] + BEFORE[0])
                        low_k(U, 1, RING_AT[0] + BEFORE[0] + 1)
                        sum_squares(tile(U, 2), False)
                        scale_qk(first_ps, 0, tile(U, 2))
                        sum_squares(tile(U, 3), False)
                        return
                    if not (first and i < 2):
                        low_att(U, i)
                    if i <= TILES and not (first and i == 0):
                        divide(U - (i == 0), (i - 1) % TILES)
                    if not (last and i >= TILES - 2) and not (first and i == 1):
                        sum_squares(tile(U, i + 2), False)
                    late = last and TILES - 2 <= i <= TILES
                    if not (first and i < 2) and not late:
                        if first and i == 2:
                            dve.wait_ge(y_free, b + 1)
                            dve.memset(y[:, TILES - 2:TILES, :], 0.0).then_inc(y_zero, 1)
                            dve.wait_ge(y_zero, b + 1)
                        add_y(U, i, first)
                    if i > TILES:
                        return
                    chunks, turns, slots = shape_of_step(i, first)
                    for k in range(slots):
                        if k < chunks and not (late and k == 1):
                            bias(U, i, k)
                        if late and k == 0:
                            if chunks:
                                bias(U, i, 1)
                            add_y(U, i, False)
                        if k < turns:
                            low_probs(U, i, k)
                        if k == 2 and not (last and i >= TILES - 2):
                            scale_qk(qkv_ps, (i + 2) % TILES, tile(U, i + 2))
                        if ahead and turns and k == turns + 1:
                            low_q(U, (i + 1) % TILES, RING_AT[i] + BEFORE[i])
                            low_k(U, (i + 1) % TILES, RING_AT[i] + BEFORE[i] + 1)

                def unit(U, first, last):
                    if first:
                        normalise_x(b, 1)
                        sum_squares(tile(U, 0), True)
                        for t in range(HT, TILES):
                            low_x(b, t)
                        scale_qk(first_ps, 0, tile(U, 0))
                        sum_squares(tile(U, 1), False)
                        low_q(U, 0, 0)
                        low_k(U, 0, 1)
                    for i in range(TILES + 2 if last else TILES):
                        step(U, i, first, last)

                units(dve, b, unit)

                def chunk(q, k, half):
                    n, c = b * CHUNKS + 2 * q + k, known(q, k)
                    dve.wait_ge(f_silu_done, n + 1)
                    if c not in (0, 1):
                        dve.wait_ge(f_high, n - 1)
                    dve.tensor_tensor(out=f_prod[k], in0=up_ps[k], in1=f_silu[k], op=ALU.mult).then_inc(f_prod_done, 1)
                    dve.wait_ge(f_high, n + 1)
                    dve.tensor_tensor(out=pT_lo[:, k, :], in0=f_prod[k], in1=pT_hi[:, k, :].bitcast(F32),
                                      op=ALU.subtract).then_inc(f_low, 1)
                    if c == FC + 2:
                        row_stats(b + 1)
                    if c == CHUNKS - 2:
                        normalise_x(b + 1, 0)
                    if c == CHUNKS - 1:
                        for t in range(HT):
                            low_x(b + 1, t)
                    for m in {FC: (0, 1), FC + 1: (2, 3), CHUNKS - 1: range(HT, TILES)}.get(c, ()):
                        dve.wait_ge(gate_done, b * TILES + m + 1)
                        dve.tensor_tensor(out=y[:, m, :], in0=y[:, m, :], in1=f_gate[m % GATES], op=ALU.mult).then_inc(gated, 1)
                        if m % HT == 0:
                            dve.wait_ge(x_again_in, (b * HALVES + m // HT + 1) * 16)
                        dve.wait_ge(gated, b * TILES + m + 1)
                        dve.tensor_tensor(out=y[:, m, :], in0=y[:, m, :], in1=x_again[:, m % HT, :], op=ALU.add).then_inc(out_ready, 1)

                feed(dve, chunk)

        @block.gpsimd
        def _(pool):
            def chained(ins, done, count):
                ins.then_inc(pool_chain, 1)
                pool.wait_ge(pool_chain, done + count)
                pool.sem_inc(pool_passed, 1)

            def rsqrt(src, at, mul, add, done):
                xx, aa, yy = rs_x[:, at], rs_a[:, at], rs_y[:, at]
                chained(pool.tensor_scalar(xx, src, mul, add, ALU.mult, ALU.add), done, 1)
                chained(pool.tensor_scalar(yy.bitcast(I32), xx.bitcast(I32), -0.5, RSQRT_SEED, ALU.mult, ALU.add), done, 2)
                chained(pool.tensor_tensor(out=aa, in0=yy, in1=yy, op=ALU.mult), done, 3)
                chained(pool.tensor_tensor(out=aa, in0=aa, in1=xx, op=ALU.mult), done, 4)
                chained(pool.tensor_scalar(aa, aa, -RSQRT_C1, RSQRT_C0, ALU.mult, ALU.add), done, 5)
                chained(pool.tensor_tensor(out=yy, in0=aa, in1=yy, op=ALU.mult), done, 6)
                chained(pool.tensor_tensor(out=aa, in0=yy, in1=yy, op=ALU.mult), done, 7)
                chained(pool.tensor_tensor(out=aa, in0=aa, in1=xx, op=ALU.mult), done, 8)
                chained(pool.tensor_scalar(xx, aa, 0.375, -1.25, ALU.mult, ALU.add), done, 9)
                chained(pool.tensor_tensor(out=aa, in0=aa, in1=xx, op=ALU.mult), done, 10)
                chained(pool.tensor_scalar(aa, aa, 1.0, 1.875, ALU.mult, ALU.add), done, 11)
                chained(pool.tensor_tensor(out=yy, in0=aa, in1=yy, op=ALU.mult), done, 12)

            def split(hi, lo, src, high, high_count, done):
                pool.sem_inc(pool_passed, 1)
                pool.tensor_copy(hi, src).then_inc(high, 1)
                pool.wait_ge(high, high_count)
                pool.tensor_tensor(out=lo, in0=src, in1=hi.bitcast(F32), op=ALU.subtract).then_inc(done, 1)

            def low_w(U, chunks=range(DC)):
                for c in chunks:
                    pool.wait_ge(w_high, U * DC + c + 1)
                    pool.tensor_tensor(out=qkv_lo[:, c, :], in0=qkv_raw[:, c, :], in1=qkv_hi[:, c, :].bitcast(F32),
                                       op=ALU.subtract).then_inc(w_split, 1)

            def low_o(U):
                for k, part in enumerate(o_parts):
                    pool.wait_ge(o_high, 2 * U + k + 1)
                    pool.tensor_tensor(out=o_lo[:, part], in0=o_raw[:, part], in1=o_hi[:, part].bitcast(F32),
                                       op=ALU.subtract).then_inc(o_split, 1)

            def x_norms(row, half):
                at = slice(half * HT, (half + 1) * HT)
                pool.wait_ge(mv_done, row * TILES + (half + 1) * HT)
                pool.sem_inc(pool_passed, 1)
                rsqrt(mv[:, at, 1], at, 1.0, LN_EPS, (row * CHAINS + half) * CHAIN)

            for half in range(HALVES):
                x_norms(0, half)
            pool.wait_ge(w_split, DC // 2)
            low_w(0, range(DC // 2, DC))
            with pool.Fori(0, B) as b:
                def low_gate_up(q, k):
                    pool.wait_ge(f_gu_high, b * CHUNKS + 2 * q + k + 1)
                    pool.tensor_tensor(out=gu_lo[k], in0=f_raw[k][:, 0:NGU], in1=gu_hi[k].bitcast(F32),
                                       op=ALU.subtract).then_inc(f_gu_split, 1)

                def low_down(q, k):
                    pool.wait_ge(f_d_high, b * CHUNKS + 2 * q + k + 1)
                    pool.tensor_tensor(out=d_lo[k], in0=f_raw[k][:, NGU:NCH], in1=d_hi[k].bitcast(F32),
                                       op=ALU.subtract).then_inc(f_d_split, 1)

                def norms(U, i):
                    t = tile(U, i)
                    if i % TILES == 0:
                        pool.wait_ge(inv_in, (U + 1 + i // TILES) * 16)
                    pool.wait_ge(summed, t)
                    pool.sem_inc(pool_passed, 1)
                    rsqrt(sq_sum[:, :], slice(TILES, TILES + G + 1), 1.0 / P, RMS_EPS, ((b + 1) * HALVES + t - 1) * CHAIN)
                    pool.tensor_tensor(out=rq[:, :], in0=rs_y[:, TILES:TILES + G + 1], in1=inv_slope[:, :], op=ALU.mult).then_inc(rq_done, 1)

                def split_v(U, i, first):
                    if i == 0 and not first:
                        pool.wait_ge(weighed, U * TURNS)
                    pool.wait_ge(v_staged, tile(U, i))
                    split(v_hi[:, i * P:(i + 1) * P], v_lo[:, i * P:(i + 1) * P], v_nat[:, i % VBUFS, :], v_high, tile(U, i), v_split)

                def step(U, i, first, last):
                    if i >= TILES:
                        low_gate_up(0, i - TILES)
                    if i == TILES:
                        low_down(0, 0)
                    if not (last and i >= TILES - 2):
                        norms(U, i + 2)
                    if i == 1:
                        low_o(U)
                    if i == TILES - 3:
                        low_w(U + 1)
                    if i < TILES:
                        split_v(U, i, first)

                def unit(U, first, last):
                    if first:
                        norms(U, 0)
                        norms(U, 1)
                    for i in range(TILES + 2 if last else TILES):
                        step(U, i, first, last)

                def chunk(q, k, half):
                    c = known(q, k)
                    if c in (0, 1):
                        return
                    low_down(q if k else q - 1, 1 - k)
                    low_gate_up(q, k)
                    if c == CHUNKS - 2:
                        x_norms(b + 1, 0)
                    if c == CHUNKS - 1:
                        low_down(q, k)
                        x_norms(b + 1, 1)

                units(pool, b, unit)
                feed(pool, chunk)


_INS = ["x", "w_qkv", "w_o", "w_ffn", "q_norm", "k_norm", "rel", "slopes", "inv_slopes", "ident"]


def kernel(L0_attn_x, L0_attn_Wq, L0_attn_Wk, L0_attn_Wv, L0_attn_Wo, L0_attn_q_norm_w, L0_attn_k_norm_w,
           L0_ffn_w_gate, L0_ffn_w_up, L0_ffn_w_down):
    import concourse.bacc as bacc
    from concourse.bass_utils import run_bass_kernel_spmd

    def by_chunk(w, parts, n):
        return np.asarray(w).reshape(parts, n, DC, P).transpose(0, 3, 2, 1).reshape(parts, P, DC * n)

    def padded(w):
        full = np.zeros((FC * P, D), np.float32)
        full[:INNER] = np.asarray(w)
        return full

    wq = by_chunk(L0_attn_Wq, HKV, G * P)
    wkv = by_chunk(np.concatenate([np.asarray(L0_attn_Wk).reshape(HKV, P, D), np.asarray(L0_attn_Wv).reshape(HKV, P, D)], 1), HKV, KV)
    ffn = np.concatenate([by_chunk(padded(L0_ffn_w_gate), FC, P), by_chunk(padded(L0_ffn_w_up), FC, P),
                          padded(np.asarray(L0_ffn_w_down).T).reshape(FC, P, D)], 2)
    p, u = np.arange(P)[:, None], np.arange(S)[None, :] - (S - P)
    start = 2.0 ** (-2.0 ** -(np.log2(H) - 3))
    slope = np.array([start * start ** i for i in range(H)], np.float32).reshape(HKV, 1, G)
    arrays = {
        "x": np.asarray(L0_attn_x),
        "w_qkv": np.concatenate([wq.reshape(HKV, P, DC, D), wkv.reshape(HKV, P, DC, KV)], 3).reshape(HKV, P, DC * NW),
        "w_o": np.asarray(L0_attn_Wo).T.reshape(HKV, G, P, D).transpose(0, 2, 1, 3).reshape(HKV, P, G * D),
        "w_ffn": ffn,
        "q_norm": np.asarray(L0_attn_q_norm_w).reshape(P, 1),
        "k_norm": np.asarray(L0_attn_k_norm_w).reshape(P, 1),
        "rel": np.where(u <= p, u - p, -MASK).astype(np.float32),
        "slopes": np.broadcast_to(-slope, (HKV, P, G)),
        "inv_slopes": np.broadcast_to(np.concatenate([1 / slope, np.ones((HKV, 1, 1), np.float32)], 2), (HKV, P, G + 1)),
        "ident": np.eye(P, dtype=np.float32),
    }
    nc = bacc.Bacc("TRN2", target_bir_lowering=False, num_devices=1)
    args, feed = [], {}
    for name in _INS:
        a = np.ascontiguousarray(arrays[name])
        feed[f"{name}_dram"] = a
        args.append(nc.dram_tensor(f"{name}_dram", a.shape, mybir.dt.from_np(a.dtype), kind="ExternalInput").ap())
    out = nc.dram_tensor("out_dram", (B, S, D), F32, kind="ExternalOutput").ap()
    build(nc, *args, out)
    got = run_bass_kernel_spmd(nc, [feed], core_ids=[0])
    return got.results[0]["out_dram"]
```
